# Optimizing a Trainium2 kernel written in Bass

```python
import numpy as np
import jax
import jax.numpy as jnp

def _softmax(x, axis=-1):
    return jax.nn.softmax(x, axis=axis)

def _gelu(x):
    return jax.nn.gelu(x, approximate=True)

def _silu(x):
    return jax.nn.silu(x)

def _sigmoid(x):
    return jax.nn.sigmoid(x)

def _layernorm(x, axis=-1, eps=1e-05):
    m = jnp.mean(x, axis=axis, keepdims=True)
    v = jnp.var(x, axis=axis, keepdims=True)
    return (x - m) / jnp.sqrt(v + eps)

def _scatter_add(tgt, idx, src, axis=0):
    return tgt.at[idx].add(src)

def _segment_sum(src, seg, n):
    return jax.ops.segment_sum(src, seg, n)
kernel_name = 'mk_hybrid_d1_jaxref_r8_50ffb7'

def setup_inputs(seed: int=0):
    np.random.seed(seed)
    _w = jnp.asarray

    def _L0_attn_a_setup():
        import jax, jax.numpy as jnp
        import numpy as np
        import math
        NUM_BUCKETS = 32
        MAX_DISTANCE = 128
        HEADS = 16
        D_MODEL = 128

        def _relative_position_bucket(rel_pos, num_buckets=NUM_BUCKETS, max_distance=MAX_DISTANCE):
            n = jnp.maximum(-rel_pos, 0)
            max_exact = num_buckets // 2
            is_small = n < max_exact
            val_large = max_exact + (jnp.log(jnp.maximum(n, 1).astype(jnp.float32) / max_exact) / math.log(max_distance / max_exact) * (num_buckets - max_exact)).astype(jnp.int32)
            val_large = jnp.minimum(val_large, num_buckets - 1)
            return jnp.where(is_small, n, val_large)
        key = jax.random.key(seed)
        ks = jax.random.split(key, 7)
        d = D_MODEL
        s = 1.0 / math.sqrt(d)
        x = jax.random.normal(ks[0], (2, 256, d), dtype=jnp.float32)
        Wq = jax.random.normal(ks[1], (d, d), dtype=jnp.float32) * s
        Wk = jax.random.normal(ks[2], (d, d), dtype=jnp.float32) * s
        Wv = jax.random.normal(ks[3], (d, d), dtype=jnp.float32) * s
        Wo = jax.random.normal(ks[4], (d, d), dtype=jnp.float32) * s
        bo = jnp.zeros((d,), dtype=jnp.float32)
        rel_emb = jax.random.normal(ks[5], (NUM_BUCKETS, HEADS), dtype=jnp.float32) * 0.02
        return {'x': x, 'Wq': Wq, 'Wk': Wk, 'Wv': Wv, 'Wo': Wo, 'bo': bo, 'rel_emb': rel_emb}
    _L0_attn_a_in = _L0_attn_a_setup()

    def _L0_attn_b_setup():
        import jax, jax.numpy as jnp
        import numpy as np
        HEADS = 16
        DIM_HEAD = 64
        ROT_DIM = 32
        SCALE = DIM_HEAD ** (-0.5)

        def _rope(x):
            n = x.shape[2]
            inv_freq = 1.0 / 10000.0 ** (jnp.arange(0, ROT_DIM, 2, dtype=jnp.float32) / ROT_DIM)
            ang = jnp.arange(n, dtype=jnp.float32)[:, None] * inv_freq[None, :]
            cos, sin = (jnp.cos(ang), jnp.sin(ang))
            x_rot, x_pass = (x[..., :ROT_DIM], x[..., ROT_DIM:])
            x1 = x_rot[..., 0::2]
            x2 = x_rot[..., 1::2]
            y1 = x1 * cos - x2 * sin
            y2 = x2 * cos + x1 * sin
            y = jnp.stack([y1, y2], axis=-1).reshape(x_rot.shape)
            return jnp.concatenate([y, x_pass], axis=-1)
        key = jax.random.key(seed)
        ks = jax.random.split(key, 5)
        b, n, d = (4, 256, 128)
        inner = HEADS * DIM_HEAD
        return {'queries': jax.random.normal(ks[0], (b, n, d), jnp.float32), 'Wq': jax.random.normal(ks[1], (d, inner), jnp.float32) * d ** (-0.5), 'Wkv': jax.random.normal(ks[2], (d, 2 * inner), jnp.float32) * d ** (-0.5), 'Wout': jax.random.normal(ks[3], (inner, d), jnp.float32) * inner ** (-0.5), 'bout': jnp.zeros((d,), jnp.float32)}
    _L0_attn_b_in = _L0_attn_b_setup()

    def _L0_ffn_setup():
        import jax, jax.numpy as jnp
        import numpy as np
        B, S, D = (4, 512, 128)
        E, F_EXP = (16, 256)
        F_C = 2.0
        F_SH = 256
        key = jax.random.key(seed)
        ks = jax.random.split(key, 8)
        s = 0.02
        return {'hidden_states': jax.random.normal(ks[0], (B, S, D), jnp.float32), 'gate_w': jax.random.normal(ks[1], (E, D), jnp.float32) * s, 'Wg': jax.random.normal(ks[2], (E, F_EXP, D), jnp.float32) * s, 'Wu': jax.random.normal(ks[3], (E, F_EXP, D), jnp.float32) * s, 'Wd': jax.random.normal(ks[4], (E, D, F_EXP), jnp.float32) * s, 'Ws_g': jax.random.normal(ks[5], (F_SH, D), jnp.float32) * s, 'Ws_u': jax.random.normal(ks[6], (F_SH, D), jnp.float32) * s, 'Ws_d': jax.random.normal(ks[7], (D, F_SH), jnp.float32) * s}
    _L0_ffn_in = _L0_ffn_setup()
    _d = {'L0_attn_a_x': _L0_attn_a_in['x'], 'L0_attn_a_Wq': _L0_attn_a_in['Wq'], 'L0_attn_a_Wk': _L0_attn_a_in['Wk'], 'L0_attn_a_Wv': _L0_attn_a_in['Wv'], 'L0_attn_a_Wo': _L0_attn_a_in['Wo'], 'L0_attn_a_bo': _L0_attn_a_in['bo'], 'L0_attn_a_rel_emb': _L0_attn_a_in['rel_emb'], 'L0_attn_b_Wq': _L0_attn_b_in['Wq'], 'L0_attn_b_Wkv': _L0_attn_b_in['Wkv'], 'L0_attn_b_Wout': _L0_attn_b_in['Wout'], 'L0_attn_b_bout': _L0_attn_b_in['bout'], 'L0_ffn_gate_w': _L0_ffn_in['gate_w'], 'L0_ffn_Wg': _L0_ffn_in['Wg'], 'L0_ffn_Wu': _L0_ffn_in['Wu'], 'L0_ffn_Wd': _L0_ffn_in['Wd'], 'L0_ffn_Ws_g': _L0_ffn_in['Ws_g'], 'L0_ffn_Ws_u': _L0_ffn_in['Ws_u'], 'L0_ffn_Ws_d': _L0_ffn_in['Ws_d']}
    _x0 = _d['L0_attn_a_x']
    _d['L0_attn_a_x'] = jax.random.normal(jax.random.fold_in(jax.random.key(seed), 1), (16, 256, 128), dtype=_x0.dtype)
    del _x0
    return _d

def reference(L0_attn_a_x, L0_attn_a_Wq, L0_attn_a_Wk, L0_attn_a_Wv, L0_attn_a_Wo, L0_attn_a_bo, L0_attn_a_rel_emb, L0_attn_b_Wq, L0_attn_b_Wkv, L0_attn_b_Wout, L0_attn_b_bout, L0_ffn_gate_w, L0_ffn_Wg, L0_ffn_Wu, L0_ffn_Wd, L0_ffn_Ws_g, L0_ffn_Ws_u, L0_ffn_Ws_d):

    def _L0_attn_a_ref(x, Wq, Wk, Wv, Wo, bo, rel_emb):
        import jax, jax.numpy as jnp
        import numpy as np
        import math
        NUM_BUCKETS = 32
        MAX_DISTANCE = 128
        HEADS = 16
        D_MODEL = 128

        def _relative_position_bucket(rel_pos, num_buckets=NUM_BUCKETS, max_distance=MAX_DISTANCE):
            n = jnp.maximum(-rel_pos, 0)
            max_exact = num_buckets // 2
            is_small = n < max_exact
            val_large = max_exact + (jnp.log(jnp.maximum(n, 1).astype(jnp.float32) / max_exact) / math.log(max_distance / max_exact) * (num_buckets - max_exact)).astype(jnp.int32)
            val_large = jnp.minimum(val_large, num_buckets - 1)
            return jnp.where(is_small, n, val_large)
        b, n, d = x.shape
        h = HEADS
        dh = d // h
        scale = dh ** (-0.5)
        q = (x @ Wq).reshape(b, n, h, dh).transpose(0, 2, 1, 3)
        k = (x @ Wk).reshape(b, n, h, dh).transpose(0, 2, 1, 3)
        v = (x @ Wv).reshape(b, n, h, dh).transpose(0, 2, 1, 3)
        sim = jnp.einsum('bhid,bhjd->bhij', q, k) * scale
        pos = jnp.arange(n, dtype=jnp.int32)
        rel_pos = pos[None, :] - pos[:, None]
        buckets = _relative_position_bucket(rel_pos)
        bias = rel_emb[buckets]
        sim = sim + jnp.transpose(bias, (2, 0, 1))[None]
        mask_value = -jnp.finfo(sim.dtype).max
        causal_mask = jnp.triu(jnp.ones((n, n), dtype=bool), k=1)
        sim = jnp.where(causal_mask[None, None], mask_value, sim)
        attn = jax.nn.softmax(sim, axis=-1)
        out = jnp.einsum('bhij,bhjd->bhid', attn, v)
        out = out.transpose(0, 2, 1, 3).reshape(b, n, d)
        return out @ Wo + bo

    def _L0_attn_b_ref(queries, Wq, Wkv, Wout, bout):
        import jax, jax.numpy as jnp
        import numpy as np
        HEADS = 16
        DIM_HEAD = 64
        ROT_DIM = 32
        SCALE = DIM_HEAD ** (-0.5)

        def _rope(x):
            n = x.shape[2]
            inv_freq = 1.0 / 10000.0 ** (jnp.arange(0, ROT_DIM, 2, dtype=jnp.float32) / ROT_DIM)
            ang = jnp.arange(n, dtype=jnp.float32)[:, None] * inv_freq[None, :]
            cos, sin = (jnp.cos(ang), jnp.sin(ang))
            x_rot, x_pass = (x[..., :ROT_DIM], x[..., ROT_DIM:])
            x1 = x_rot[..., 0::2]
            x2 = x_rot[..., 1::2]
            y1 = x1 * cos - x2 * sin
            y2 = x2 * cos + x1 * sin
            y = jnp.stack([y1, y2], axis=-1).reshape(x_rot.shape)
            return jnp.concatenate([y, x_pass], axis=-1)
        b, n, _ = queries.shape
        q = queries @ Wq
        kv = queries @ Wkv
        k, v = jnp.split(kv, 2, axis=-1)
        split_heads = lambda t: t.reshape(b, n, HEADS, DIM_HEAD).transpose(0, 2, 1, 3)
        q, k, v = (split_heads(q), split_heads(k), split_heads(v))
        q, k = (_rope(q), _rope(k))
        sim = jnp.einsum('bhid,bhjd->bhij', q, k) * SCALE
        attn = jax.nn.softmax(sim, axis=-1)
        out = jnp.einsum('bhij,bhjd->bhid', attn, v)
        out = out.transpose(0, 2, 1, 3).reshape(b, n, HEADS * DIM_HEAD)
        return out @ Wout + bout

    def _L0_ffn_ref(hidden_states, gate_w, Wg, Wu, Wd, Ws_g, Ws_u, Ws_d):
        import jax, jax.numpy as jnp
        import numpy as np
        B, S, D = (4, 512, 128)
        E, F_EXP = (16, 256)
        F_C = 2.0
        F_SH = 256
        b, s, d = hidden_states.shape
        e = gate_w.shape[0]
        cap = int(s * F_C / e)
        logits = jnp.einsum('bsd,ed->bse', hidden_states, gate_w)
        scores = jax.nn.softmax(logits, axis=-1).transpose(0, 2, 1)
        topk_w, topk_idx = jax.lax.top_k(scores, cap)
        x_tok = jnp.take_along_axis(hidden_states[:, None, :, :], topk_idx[..., None], axis=2)
        g = jnp.einsum('becd,efd->becf', x_tok, Wg)
        u = jnp.einsum('becd,efd->becf', x_tok, Wu)
        h = jax.nn.gelu(g, approximate=False) * u
        eo = jnp.einsum('becf,edf->becd', h, Wd) * topk_w[..., None]
        offs = (jnp.arange(b) * s)[:, None, None]
        flat_idx = (topk_idx + offs).reshape(-1)
        flat = jnp.zeros((b * s, d), hidden_states.dtype)
        flat = flat.at[flat_idx].add(eo.reshape(-1, d))
        out = flat.reshape(b, s, d)
        gs = jnp.einsum('bsd,fd->bsf', hidden_states, Ws_g)
        us = jnp.einsum('bsd,fd->bsf', hidden_states, Ws_u)
        shared = jnp.einsum('bsf,df->bsd', jax.nn.gelu(gs, approximate=False) * us, Ws_d)
        return out + shared
    x = L0_attn_a_x
    x = x + _L0_attn_a_ref(_layernorm(x, axis=-1), L0_attn_a_Wq, L0_attn_a_Wk, L0_attn_a_Wv, L0_attn_a_Wo, L0_attn_a_bo, L0_attn_a_rel_emb)
    x = x + _L0_ffn_ref(_layernorm(x, axis=-1), L0_ffn_gate_w, L0_ffn_Wg, L0_ffn_Wu, L0_ffn_Wd, L0_ffn_Ws_g, L0_ffn_Ws_u, L0_ffn_Ws_d)
    x = x + _L0_attn_b_ref(_layernorm(x, axis=-1), L0_attn_b_Wq, L0_attn_b_Wkv, L0_attn_b_Wout, L0_attn_b_bout)
    x = x + _L0_ffn_ref(_layernorm(x, axis=-1), L0_ffn_gate_w, L0_ffn_Wg, L0_ffn_Wu, L0_ffn_Wd, L0_ffn_Ws_g, L0_ffn_Ws_u, L0_ffn_Ws_d)
    return x

_drawn_inputs = setup_inputs


def setup_inputs(seed=0):
    import zlib

    import numpy as np

    out = dict(_drawn_inputs(seed))
    spreads = {'L0_attn_a_bo': (0.0, 0.1), 'L0_attn_b_bout': (0.0, 0.1)}
    factors = {'L0_attn_a_rel_emb': 8.0,
     'L0_ffn_gate_w': 8.0,
     'L0_ffn_Wg': 8.0,
     'L0_ffn_Wu': 8.0,
     'L0_ffn_Wd': 8.0,
     'L0_ffn_Ws_g': 3.611,
     'L0_ffn_Ws_u': 3.548,
     'L0_ffn_Ws_d': 3.559}
    for name, (base, spread) in spreads.items():
        noise = np.random.default_rng([zlib.crc32(name.encode()), seed]).standard_normal(out[name].shape)
        drawn = base * np.exp(spread * noise) if base else spread * noise
        out[name] = jnp.asarray(drawn.astype(out[name].dtype))
    for name, factor in factors.items():
        out[name] = (out[name] * factor).astype(out[name].dtype)
    return out
```

```python
import math
from contextlib import ExitStack, contextmanager

import numpy as np
import concourse.bass as bass
from concourse import mybir

F32 = mybir.dt.float32
F32R = mybir.dt.float32r
BF16 = mybir.dt.bfloat16
ALU = mybir.AluOpType
ACT = mybir.ActivationFunctionType
AX = mybir.AxisListType

NB = 16
N = 256
D = 128
NH = 2
NT = NB * NH
EPS = 1e-5
BIG = 1.0e38


@contextmanager
def semaphores(nc, tag, names):
    held = {n: nc.alloc_semaphore(tag + n) for n in names.split()}
    yield held
    nc.clear_and_free_semaphores(list(held.values()))
    nc.all_engine_barrier()


def need(eng, sem, value):
    if isinstance(value, int) and value <= 0:
        return
    eng.wait_ge(sem, value)


def values(eng, *terms):
    return [t if isinstance(t, int) else eng.snap(t) for t in terms]


def stats_tiles(nc, dve, chain, x, b, stat, mv, gate):
    for half in range(NH):
        chain.link(nc.vector.bn_stats(stat[:, half, :], x[:, 2 * b + half, :]))
    chain.reach()
    chain.link(nc.vector.memset(gate[:, :], 0.0))
    for half in range(NH):
        last = nc.vector.bn_aggr(mv[:, half, :], stat[:, half, :])
    return last


def rstd_tiles(nc, pool, mv, consts, rstd, added, count):
    two = lambda c: consts[:, c:c + 1].broadcast_to([128, NH])
    nc.gpsimd.tensor_tensor(rstd[:, 0, :], mv[:, :, 1], two(0), ALU.add).then_inc(added, 1)
    pool.wait_ge(added, count)
    return nc.gpsimd.tensor_tensor(rstd[:, 1, :], rstd[:, 0, :], two(1), ALU.pow)


def norm_tiles(nc, x, b, mv, rstd, xn):
    for half in range(NH):
        last = nc.vector.tensor_scalar(xn[:, half, :], x[:, 2 * b + half, :], mv[:, half, 0:1],
                                       rstd[:, 1, half:half + 1], ALU.subtract, ALU.mult)
    return last


class Chain:

    def __init__(self, eng, sem, links, batch):
        self.eng, self.sem, self.links, self.base, self.n = eng, sem, links, batch * links, 0

    def link(self, ins):
        self.n += 1
        ins.then_inc(self.sem, 1)

    def reach(self, n=None):
        self.eng.wait_ge(self.sem, self.base + (self.n if n is None else n))

    def close(self):
        assert self.n == self.links, (self.n, self.links)


def causal_attention(nc, ctx, x, ident, x_in, wq, wk, wv, wo, bo, rel_emb, buckets):
    H, DH = 16, 8
    GROUPS, GH = 4, 4
    SCALE = DH ** -0.5
    LT, LP, LN_ = 3, 6, 7
    PARTS = [(0, 0), (0, 1), (0, 2), (1, 0), (1, 1), (2, 0)]
    RUNS = [[(m, 1) for m in range(6)], [(0, 3), (3, 2), (5, 1)]]
    KR = DH * len(PARTS)

    def sb(name, shape, dt=F32):
        return ctx.enter_context(nc.sbuf_tensor("a_" + name, shape, dt))

    def bank(name):
        return ctx.enter_context(nc.psum_tensor("a_" + name, [128, 512], F32))

    w_in = sb("w_in", [128, 4, D])
    w_hi, w_lo = sb("w_hi", [128, 3, D], F32R), sb("w_lo", [128, 3, D], F32R)
    bo_all = sb("bo_all", [128, D])
    rel = sb("rel", [64, H])
    hot = sb("hot", [64, 384])
    dist_bias = sb("dist_bias", [H, 384])
    bias = sb("bias", [128, H, 256])
    stat, mv, rstd = sb("stat", [128, NH, 6]), sb("mv", [128, NH, 2]), sb("rstd", [128, 2, NH])
    gate, gate2, consts = sb("gate", [128, 1]), sb("gate2", [1, 4]), sb("consts", [128, 2])
    xn = sb("xn", [128, NH, D])
    xt_hi, xt_lo = sb("xt_hi", [128, N], F32R), sb("xt_lo", [128, N], F32R)
    part = [sb(f"part{n}", [128, 2 * N], BF16) for n in range(3)]
    rest = sb("rest", [128, 2 * N])
    qk_pack = [[sb(f"pack{s}{u}", [KR, H, N], BF16) for u in range(2)] for s in range(2)]
    v_pad = [sb(f"v_pad{u}", [128, NH, H, 32]) for u in range(2)]
    prob = [sb(f"prob{n}", [128, 384]) for n in range(4)]
    shift = sb("shift", [128, 4, 2])
    prob_t = [sb(f"prob_t{n}", [128, 384]) for n in range(8)]
    o_t = sb("o_t", [128, N])
    r_sum = sb("r_sum", [128, NH, GH])
    o = sb("o", [128, NH, D])
    of_t = sb("of_t", [128, N])
    parts = nc.dram_tensor("a_parts", (2, 2, H, 3, DH, N), BF16)
    parts_dram = parts.ap()
    SKEW = 8
    scratch = nc.dram_tensor("a_bias_by_distance", (SKEW, H, 384), F32)

    S, PT = [bank("S0"), bank("S1")], [bank("PT0"), bank("PT1")]
    OT, ON, QK, M = bank("OT"), bank("ON"), bank("QK"), bank("M")

    names = ("w_loaded rel_loaded hot_loaded x0_loaded x_loaded bo_loaded w_split dist_done dist_copied dist_stored "
             "bias_loaded v_cleared prep mv veps rstd sc mx ex tr ptv pta ot ots on o of ofs wo x_done xn_r xt xth xtl qk q1 rs q2 q3 kept "
             "packed v vs xb msk norm")
    s = ctx.enter_context(semaphores(nc, "a_", names))
    NDMA = 9
    ev_act = lambda h: h % 4 == 3
    N_EV_ACT = 4
    X_STEP = 2
    LOOPS = (NB - 2) // 2

    def stepper(eng, iteration):
        iteration(0, 0, True, True)
        with eng.Fori(0, LOOPS) as i:
            for u in range(2):
                iteration(2 * i + 1 + u, (1 + u) % 2, True, True)
        iteration(NB - 1, (NB - 1) % 2, True, False)
        iteration(NB, NB % 2, False, False)

    def lagged(b, step, lag):
        return (b, step - lag) if step >= lag else (b - 1, step - lag + H)

    def real(b):
        return not (isinstance(b, int) and b < 0)

    blk = ctx.enter_context(nc.Block())

    @blk.sync
    def _(sp):
        for n, w in enumerate((wq, wk, wv, wo)):
            sp.dma_start(w_in[:, n, :], w).then_inc(s["w_loaded"], 16)
        x_tiles = x_in.rearrange("b (t p) d -> p (b t) d", p=128)
        sp.dma_start(x[:, 0:2, :], x_tiles[:, 0:2, :]).then_inc(s["x0_loaded"], 16)
        sp.dma_start(rel[0:32, :], rel_emb).then_inc(s["rel_loaded"], 16)
        sp.dma_start(hot[0:33, :], buckets).then_inc(s["hot_loaded"], 16)
        sp.dma_start(x[:, 2:NT, :], x_tiles[:, 2:NT, :]).then_inc(s["x_loaded"], 16)
        sp.dma_start(bo_all[:, :], bo.rearrange("(a d) -> a d", a=1).broadcast_to([128, D])).then_inc(s["bo_loaded"], 16)
        sp.wait_ge(s["dist_copied"], 1)
        sp.dma_start(scratch.ap().rearrange("r h u -> h r u"),
                     dist_bias[:, :].rearrange("h (a u) -> h a u", a=1).broadcast_to([H, SKEW, 384])).then_inc(s["dist_stored"], 16)
        sp.wait_ge(s["dist_stored"], 16)
        for i in range(0, 128, SKEW):
            skewed = bass.AP(tensor=scratch, offset=127 - i, ap=[[H * 384 - 1, SKEW], [384, H], [1, 256]])
            sp.dma_start(bias[i:i + SKEW, :, :], skewed).then_inc(s["bias_loaded"], 16)

        def pack(b, par):
            def load(side, runs):
                for m, count in runs:
                    src = bass.AP(tensor=parts, offset=((par * 2 + side) * 128 * 3 + DH * PARTS[m][side]) * N,
                                  ap=[[N, DH * count], [3 * DH * N, H], [1, N]])
                    sp.dma_start(qk_pack[side][par][DH * m:DH * (m + count), :, :], src).then_inc(s["packed"], 16)

            for p, ready in ((0, "q1"), (1, "q2"), (2, "q3")):
                sp.wait_ge(s[ready], b + 1)
                for side in range(2):
                    sp.dma_start(parts_dram[par, side, :, p, :, :], part[p][:, N * side:N * side + N]).then_inc(s["kept"], 16)
                if p == 0:
                    sp.wait_ge(s["kept"], 96 * b + 32)
                    load(0, RUNS[0][0:3])
            sp.wait_ge(s["kept"], 96 * (b + 1))
            load(0, RUNS[0][3:])
            load(1, RUNS[1])

        pack(0, 0)

        def iteration(b, par, attend, prep):
            if prep:
                pack(b + 1, 1 - par)
        stepper(sp, iteration)

    @blk.gpsimd
    def _(pool):
        for u in range(2):
            nc.gpsimd.memset(v_pad[u][:, :, :, 0:DH], 0.0)
            nc.gpsimd.memset(v_pad[u][:, :, :, DH + 1:32], 0.0)
            last = nc.gpsimd.memset(v_pad[u][:, :, :, DH:DH + 1], 1.0)
        last.then_inc(s["v_cleared"], 1)
        nc.gpsimd.memset(consts[:, 0:1], EPS)
        nc.gpsimd.memset(consts[:, 1:2], -0.5).then_inc(s["v_cleared"], 1)
        pool.wait_ge(s["v_cleared"], 2)
        nc.gpsimd.memset(rel[32:64, :], -BIG).then_inc(s["msk"], 1)

        def prep_r(b):
            pool.wait_ge(s["mv"], b + 1)
            rstd_tiles(nc, pool, mv, consts, rstd, s["veps"], b + 1).then_inc(s["rstd"], 1)

        def prep(b):
            pool.wait_ge(s["q2"], b + 1)
            if not (isinstance(b, int) and b == 0):
                pool.wait_ge(s["kept"], 96 * b)
            nc.gpsimd.tensor_tensor(part[2][:, :], rest[:, :], part[1][:, :], ALU.subtract).then_inc(s["q3"], 1)
            pool.wait_ge(s["bo_loaded"], 16)
            pool.wait_ge(s["xn_r"], b + 1)
            nc.gpsimd.tensor_tensor(x[:, bass.ds(2 * b, 2), :], x[:, bass.ds(2 * b, 2), :],
                                    bo_all[:, :].rearrange("p (a d) -> p a d", a=1).broadcast_to([128, NH, D]),
                                    ALU.add).then_inc(s["xb"], 1)
        prep_r(0)
        prep(0)

        def iteration(b, par, attend, pr):
            if pr:
                prep_r(b + 1)
                prep(b + 1)
        stepper(pool, iteration)

    @blk.tensor
    def _(pe):
        pe.wait_ge(s["rel_loaded"], 16)
        pe.wait_ge(s["hot_loaded"], 16)
        pe.wait_ge(s["msk"], 1)
        nc.tensor.matmul(M[0:H, 0:384], rel[0:33, :], hot[0:33, :], start=True, stop=True).then_inc(s["dist_done"], 1)

        def transpose_x(b):
            pe.wait_ge(s["xn_r"], b + 1)
            if isinstance(b, int) and b == 0:
                pe.wait_ge(s["dist_copied"], 1)
            need(pe, s["x_done"], b - 2)
            for half in range(NH):
                last = nc.tensor.transpose(M[:, 128 * half:128 * half + 128], xn[:, half, :], ident[:, :])
            last.then_inc(s["xt"], 1)

        def project(b):
            pe.wait_ge(s["w_split"], 2)
            pe.wait_ge(s["xtl"], b + 1)
            need(pe, s["rs"], b)
            for side in range(2):
                out = QK[:, N * side:N * side + N]
                nc.tensor.matmul(out, w_hi[:, side, :], xt_hi[:, :], start=True, stop=False)
                nc.tensor.matmul(out, w_hi[:, side, :], xt_lo[:, :], start=False, stop=False)
                last = nc.tensor.matmul(out, w_lo[:, side, :], xt_hi[:, :], start=False, stop=True)
            last.then_inc(s["qk"], 1)

        def project_v(b):
            for half in range(NH):
                out, cols = M[:, D * half:D * half + D], slice(128 * half, 128 * half + 128)
                nc.tensor.matmul(out, xt_hi[:, cols], w_hi[:, 2, :], start=True, stop=False)
                nc.tensor.matmul(out, xt_lo[:, cols], w_hi[:, 2, :], start=False, stop=False)
                last = nc.tensor.matmul(out, xt_hi[:, cols], w_lo[:, 2, :], start=False, stop=True)
            last.then_inc(s["v"], 1)

        def scores(b, par, h):
            if h == 0:
                pe.wait_ge(s["packed"], 16 * NDMA * (b + 1))
            need(pe, s["mx"], H * b + h - 1)
            q, k = qk_pack[0][par][:, h, :], qk_pack[1][par][:, h, :]
            nc.tensor.matmul(S[h % 2][:, 0:128], q[:, 0:128], k[:, 0:128], start=True, stop=True)
            nc.tensor.matmul(S[h % 2][:, 128:384], q[:, 128:256], k[:, :], start=True, stop=True).then_inc(s["sc"], 1)

        def transpose_p(b, h):
            pe.wait_ge(s["ex"], H * b + h + 1)
            if h >= 2:
                g, n = h - 2, b
            else:
                g, n = h + H - 2, b - 1
            if real(n):
                if ev_act(g):
                    need(pe, s["pta"], N_EV_ACT * n + g // 4 + 1)
                else:
                    need(pe, s["ptv"], (H - N_EV_ACT) * n + g - g // 4 + 1)
            for c in range(3):
                last = nc.tensor.transpose(PT[h % 2][:, TB[c]:TB[c] + 128], prob[h % 4][:, 128 * c:128 * c + 128],
                                           ident[:, :])
            last.then_inc(s["tr"], 1)
        TB = (0, 128, 256)

        def attend_v(b, par, j):
            pe.wait_ge(s["pta"], N_EV_ACT * b + j + 1)
            pe.wait_ge(s["ptv"], (H - N_EV_ACT) * b + 3 * j + 3)
            if j == 0:
                pe.wait_ge(s["vs"], b + 1)
            need(pe, s["ots"], GROUPS * b + j)
            for kt, cols, src in ((0, slice(0, 256), slice(0, 256)), (1, slice(128, 256), slice(256, 384))):
                for g in range(GH):
                    h = GH * j + g
                    last = nc.tensor.matmul(OT[32 * g:32 * g + 32, cols], v_pad[par][:, kt, h, :],
                                            prob_t[h % 8][:, src], start=(kt == 0), stop=(kt == 1))
            last.then_inc(s["ot"], 1)

        def turn_o(b, j):
            pe.wait_ge(s["ots"], GROUPS * b + j + 1)
            need(pe, s["o"], GROUPS * b + j)
            for half in range(NH):
                last = nc.tensor.transpose(ON[:, 128 * half:128 * half + 128], o_t[:, 128 * half:128 * half + 128],
                                           ident[:, :])
            last.then_inc(s["on"], 1)

        def turn_back(b, free_of):
            pe.wait_ge(s["o"], GROUPS * (b + 1))
            need(pe, s["vs"], free_of)
            for half in range(NH):
                last = nc.tensor.transpose(M[:, 128 * half:128 * half + 128], o[:, half, :], ident[:, :])
            last.then_inc(s["of"], 1)

        def project_out(b):
            pe.wait_ge(s["ofs"], b + 1)
            for half in range(NH):
                last = nc.tensor.matmul(M[:, D * half:D * half + D], of_t[:, 128 * half:128 * half + 128],
                                        w_in[:, 3, :], start=True, stop=True)
            last.then_inc(s["wo"], 1)

        transpose_x(0)
        project(0)
        project_v(0)

        def iteration(b, par, attend, prep):
            for step in range(H if attend else 12):
                if attend:
                    scores(b, par, step)
                n, h = lagged(b, step, LT)
                if real(n) and (attend or step < LT):
                    transpose_p(n, h)
                n, h = lagged(b, step, LP)
                if h % 4 == 3 and real(n) and (attend or step < LP):
                    attend_v(n, par if step >= LP else 1 - par, h // 4)
                n, h = lagged(b, step, LN_)
                if h % 4 == 3 and real(n) and (attend or step < LN_):
                    turn_o(n, h // 4)
                if step == X_STEP and prep:
                    transpose_x(b + 1)
                if step == X_STEP + 2 and prep:
                    project(b + 1)
                if step == X_STEP + 3 and prep:
                    project_v(b + 1)
                if step == 9 and real(b - 1):
                    turn_back(b - 1, b + 2 if prep else 0)
                if step == 11 and real(b - 1):
                    project_out(b - 1)
        stepper(pe, iteration)

    @blk.scalar
    def _(act):
        def prep_a(b):
            act.wait_ge(s["xt"], b + 1)
            need(act, s["v"], b)
            nc.scalar.copy(xt_hi[:, :], M[:, 0:N]).then_inc(s["xth"], 1)

        def prep_b(b):
            act.wait_ge(s["qk"], b + 1)
            need(act, s["kept"], 96 * b)
            nc.scalar.copy(part[0][:, :], QK[:, :]).then_inc(s["q1"], 1)

        def prep_c(b, par):
            act.wait_ge(s["v"], b + 1)
            if isinstance(b, int) and b == 0:
                act.wait_ge(s["v_cleared"], 2)
            need(act, s["ot"], GROUPS * (b - 1))
            nc.scalar.copy(v_pad[par][:, :, :, 0:DH],
                           M[:, 0:NH * D].rearrange("p (t h r) -> p t h r", t=NH, r=DH)).then_inc(s["vs"], 1)

        def prep_d(b):
            act.wait_ge(s["rs"], b + 1)
            nc.scalar.copy(part[1][:, :], rest[:, :]).then_inc(s["q2"], 1)

        def exps(b, h):
            act.wait_ge(s["mx"], H * b + h + 1)
            nc.scalar.activation(prob[h % 4][:, 0:128], prob[h % 4][:, 0:128], ACT.Exp, bias=shift[:, h % 4, 0:1], scale=-1.0)
            nc.scalar.activation(prob[h % 4][:, 128:384], prob[h % 4][:, 128:384], ACT.Exp, bias=shift[:, h % 4, 1:2],
                                 scale=-1.0).then_inc(s["ex"], 1)

        def copy_p(b, h):
            act.wait_ge(s["tr"], H * b + h + 1)
            if h >= 8:
                need(act, s["ot"], GROUPS * b + (h - 8) // 4 + 1)
            else:
                need(act, s["ot"], GROUPS * (b - 1) + (h + 8) // 4 + 1)
            nc.scalar.copy(prob_t[h % 8][:, :], PT[h % 2][:, 0:384]).then_inc(s["pta"], 1)

        def copy_o(b, j):
            act.wait_ge(s["ot"], GROUPS * b + j + 1)
            need(act, s["on"], GROUPS * b + j)
            nc.scalar.copy(o_t[:, :], OT[:, 0:N]).then_inc(s["ots"], 1)

        prep_a(0)
        prep_b(0)
        prep_c(0, 0)
        prep_d(0)

        def iteration(b, par, attend, prep):
            for step in range(H if attend else 12):
                if attend:
                    exps(b, step)
                n, h = lagged(b, step, LT)
                if ev_act(h) and real(n) and (attend or step < LT):
                    copy_p(n, h)
                n, h = lagged(b, step, LP)
                if h % 4 == 3 and real(n) and (attend or step < LP):
                    copy_o(n, h // 4)
                if prep:
                    if step == X_STEP:
                        prep_a(b + 1)
                    if step == X_STEP + 2:
                        prep_b(b + 1)
                    if step == X_STEP + 4:
                        prep_d(b + 1)
                        prep_c(b + 1, 1 - par)
                if step == 9 and real(b - 1):
                    act.wait_ge(s["of"], b)
                    nc.scalar.copy(of_t[:, :], M[:, 0:N]).then_inc(s["ofs"], 1)
        stepper(act, iteration)

    @blk.vector
    def _(dve):
        dve.wait_ge(s["w_loaded"], 64)
        nc.vector.tensor_copy(w_hi[:, :, :], w_in[:, 0:3, :]).then_inc(s["w_split"], 1)
        dve.wait_ge(s["w_split"], 1)
        nc.vector.tensor_tensor(w_lo[:, :, :], w_in[:, 0:3, :], w_hi[:, :, :].bitcast(F32), ALU.subtract).then_inc(s["w_split"], 1)
        dve.wait_ge(s["dist_done"], 1)
        nc.vector.tensor_scalar(dist_bias[:, :], M[0:H, 0:384], 1.0 / SCALE, None, ALU.mult).then_inc(s["dist_copied"], 1)
        dve.wait_ge(s["x0_loaded"], 16)

        def prep_a(b):
            chain = Chain(dve, s["prep"], 3, b)
            need(dve, s["xb"], b)
            stats_tiles(nc, dve, chain, x, b, stat, mv, gate).then_inc(s["mv"], 1)
            chain.close()

        def prep_n(b):
            dve.wait_ge(s["rstd"], b + 1)
            need(dve, s["xt"], b)
            norm_tiles(nc, x, b, mv, rstd, xn).then_inc(s["xn_r"], 1)

        def prep_b(b):
            dve.wait_ge(s["xth"], b + 1)
            nc.vector.tensor_tensor(xt_lo[:, :], M[:, 0:N], xt_hi[:, :].bitcast(F32), ALU.subtract).then_inc(s["xtl"], 1)

        def prep_c(b):
            dve.wait_ge(s["q1"], b + 1)
            need(dve, s["q3"], b)
            nc.vector.tensor_tensor(rest[:, :], QK[:, :], part[0][:, :], ALU.subtract).then_inc(s["rs"], 1)

        def add_bias(b, h):
            dve.wait_ge(s["sc"], H * b + h + 1)
            need(dve, s["tr"], H * b + h - 3)
            nc.vector.memset(gate2[:, h % 4:h % 4 + 1], 0.0)
            nc.vector.tensor_tensor_reduce(out=prob[h % 4][:, 0:128], in0=S[h % 2][:, 0:128], in1=bias[:, h, 128:256],
                                           scale=-SCALE, scalar=BIG, op0=ALU.add, op1=ALU.min,
                                           accum_out=shift[:, h % 4, 0:1])
            nc.vector.tensor_tensor_reduce(out=prob[h % 4][:, 128:384], in0=S[h % 2][:, 128:384], in1=bias[:, h, :],
                                           scale=-SCALE, scalar=BIG, op0=ALU.add, op1=ALU.min,
                                           accum_out=shift[:, h % 4, 1:2]).then_inc(s["mx"], 1)

        def copy_p(b, h):
            dve.wait_ge(s["tr"], H * b + h + 1)
            if h >= 8:
                need(dve, s["ot"], GROUPS * b + (h - 8) // 4 + 1)
            else:
                need(dve, s["ot"], GROUPS * (b - 1) + (h + 8) // 4 + 1)
            nc.vector.tensor_copy(prob_t[h % 8][:, :], PT[h % 2][:, 0:384]).then_inc(s["ptv"], 1)

        def normalise(b, j):
            dve.wait_ge(s["on"], GROUPS * b + j + 1)
            turned = ON[:, 0:NH * 128].rearrange("p (t g r) -> p t g r", t=NH, g=GH)
            nc.vector.reciprocal(r_sum[:, :, :], turned[:, :, :, DH]).then_inc(s["norm"], 1)
            dve.wait_ge(s["norm"], GROUPS * b + j + 1)
            if j == 0:
                need(dve, s["of"], b)
            nc.vector.tensor_tensor(
                o[:, :, GH * DH * j:GH * DH * (j + 1)].rearrange("p t (g r) -> p t g r", g=GH), turned[:, :, :, 0:DH],
                r_sum[:, :, :].rearrange("p t (g a) -> p t g a", a=1).broadcast_to([128, NH, GH, DH]),
                ALU.mult).then_inc(s["o"], 1)

        prep_a(0)
        prep_n(0)
        dve.wait_ge(s["x_loaded"], 16)
        prep_b(0)
        prep_c(0)
        dve.wait_ge(s["bias_loaded"], 16 * 128 // SKEW)

        def iteration(b, par, attend, prep):
            for step in range(H if attend else 12):
                if attend:
                    add_bias(b, step)
                n, h = lagged(b, step, LT)
                if not ev_act(h) and real(n) and (attend or step < LT):
                    copy_p(n, h)
                n, h = lagged(b, step, LN_)
                if h % 4 == 3 and real(n) and (attend or step < LN_):
                    normalise(n, h // 4)
                if prep:
                    if step == 0:
                        prep_a(b + 1)
                    if step == 1:
                        prep_n(b + 1)
                    if step == X_STEP + 1:
                        prep_b(b + 1)
                    if step == X_STEP + 3:
                        prep_c(b + 1)
                if step == 11 and real(b - 1):
                    dve.wait_ge(s["wo"], b)
                    dve.wait_ge(s["xb"], b)
                    tiles = bass.ds(2 * (b - 1), 2)
                    nc.vector.tensor_tensor(x[:, tiles, :], x[:, tiles, :], M[:, 0:N].rearrange("p (t d) -> p t d", t=NH),
                                            ALU.add).then_inc(s["x_done"], 1)
        stepper(dve, iteration)


def pipelined(eng, iteration, count, depth, lead):
    for it in range(lead):
        iteration(it, it % 2)
    with eng.Fori(0, (count - lead) // 2) as i:
        for u in range(2):
            iteration(2 * i + (lead + u), u)
    for it in range(count, count + depth):
        iteration(it, it % 2)


def within(b, count):
    return not isinstance(b, int) or 0 <= b < count


def expert_choice_ffn(nc, tag, x, ident, gate_w, wg, wu, wd, ws_g, ws_u, ws_d, slots):
    E, F, CAP = 16, 256, 32
    FT = F // 128
    EC = E * CAP
    JE = 128 // CAP
    NJ = E // JE
    BG = 128 // E
    NG = NB // BG

    with ExitStack() as ctx:
        def sb(name, shape, dt=F32):
            return ctx.enter_context(nc.sbuf_tensor(tag + name, shape, dt))

        logits = sb("logits", [128, NH, NB, E])
        weight = sb("weight", [128, NH, NB, E])
        place = sb("place", [128, NH, NB, E])
        slot = sb("slot", [128, CAP])
        xn_all = sb("xn_all", [128, NT, D])

        with ExitStack() as sub:
            normalise_and_share(nc, tag + "s_", sub, x, ident, gate_w, ws_g, ws_u, ws_d, slots, logits, xn_all, slot,
                                E, F, FT, CAP)
        with ExitStack() as sub:
            route(nc, tag + "r_", sub, ident, logits, weight, place, E, CAP, BG, NG)
        with ExitStack() as mid:
            eo_all = mid.enter_context(nc.sbuf_tensor(tag + "eo_all", [128, NB, NJ, D], F32))
            with ExitStack() as sub:
                xg_hi = sub.enter_context(nc.sbuf_tensor(tag + "xg_hi", [128, E, NB, CAP], F32R))
                xg_lo = sub.enter_context(nc.sbuf_tensor(tag + "xg_lo", [128, E, NB, CAP], F32R))
                with ExitStack() as inner:
                    gather(nc, tag + "g_", inner, xn_all, place, slot, xg_hi, xg_lo, E, CAP)
                with ExitStack() as inner:
                    experts(nc, tag + "e_", inner, xg_hi, xg_lo, wg, wu, wd, eo_all, E, F, FT, CAP)
            with ExitStack() as sub:
                combine(nc, tag + "c_", sub, x, ident, place, weight, slot, eo_all, E, CAP, NJ)


def normalise_and_share(nc, tag, ctx, x, ident, gate_w, ws_g, ws_u, ws_d, slots, logits, xn_all, slot, E, F, FT, CAP):
    sb = lambda name, shape, dt=F32: ctx.enter_context(nc.sbuf_tensor(tag + name, shape, dt))
    bank = lambda name: ctx.enter_context(nc.psum_tensor(tag + name, [128, 512], F32))
    C = 2 * F + E
    w_in, w_hi, w_lo = sb("w_in", [128, C]), sb("w_hi", [128, C], F32R), sb("w_lo", [128, C], F32R)
    w_down = sb("w_down", [128, FT, D])
    consts, gate = sb("consts", [128, 2]), sb("gate", [128, 1])
    stat, mv, rstd = sb("stat", [128, NH, 6]), sb("mv", [128, 2, NH, 2]), sb("rstd", [128, 2, 2, NH])
    xn = [sb(f"xn{u}", [128, NH, D]) for u in range(2)]
    xt_hi = [sb(f"xt_hi{u}", [128, N], F32R) for u in range(2)]
    xt_lo = [sb(f"xt_lo{u}", [128, N], F32R) for u in range(2)]
    act_g = [sb(f"act_g{u}", [128, FT, N]) for u in range(2)]
    hid = [sb(f"hid{u}", [128, FT, N]) for u in range(2)]
    XT, G, U = ([bank(n + str(u)) for u in range(2)] for n in ("XT", "G", "U"))
    L, Y = bank("L"), bank("Y")
    names = "w_loaded d_loaded split ready mv veps rstd prep xn kept xt xth xtl gu lg lgc gel hid y xadd"
    s = ctx.enter_context(semaphores(nc, tag, names))
    blk = ctx.enter_context(nc.Block())
    DEPTH, LEAD = 5, 6

    @blk.sync
    def _(sp):
        for src, at in ((ws_g, 0), (ws_u, F), (gate_w, 2 * F)):
            sp.dma_start(w_in[:, at:at + src.shape[1]], src).then_inc(s["w_loaded"], 16)
        sp.dma_start(slot[:, :], slots.rearrange("(a c) -> a c", a=1).broadcast_to([128, CAP])).then_inc(s["d_loaded"], 16)
        sp.dma_start(w_down[:, :, :], ws_d.rearrange("(t p) d -> p t d", p=128)).then_inc(s["d_loaded"], 16)

    @blk.gpsimd
    def _(pool):
        nc.gpsimd.memset(consts[:, 0:1], EPS)
        nc.gpsimd.memset(consts[:, 1:2], -0.5).then_inc(s["ready"], 1)
        pool.wait_ge(s["ready"], 1)

        def iteration(it, par):
            if within(it, NB):
                pool.wait_ge(s["mv"], it + 1)
                need(pool, s["xn"], it - 1)
                rstd_tiles(nc, pool, mv[:, par], consts, rstd[:, par], s["veps"], it + 1).then_inc(s["rstd"], 1)
            b = it - 1
            if within(b, NB):
                pool.wait_ge(s["xn"], b + 1)
                nc.gpsimd.tensor_copy(xn_all[:, bass.ds(2 * b, NH), :], xn[1 - par][:, :, :]).then_inc(s["kept"], 1)
        pipelined(pool, iteration, NB, DEPTH, LEAD)
        pool.wait_ge(s["kept"], NB)

    @blk.vector
    def _(dve):
        def iteration(it, par):
            b = it - 5
            if within(b, NB):
                dve.wait_ge(s["y"], b + 1)
                nc.vector.tensor_tensor(x[:, bass.ds(2 * b, NH), :], x[:, bass.ds(2 * b, NH), :],
                                        Y[:, 0:N].rearrange("p (t d) -> p t d", t=NH), ALU.add).then_inc(s["xadd"], 1)
            b = it - 4
            if within(b, NB):
                dve.wait_ge(s["gel"], b + 1)
                need(dve, s["y"], b - 1)
                nc.vector.tensor_tensor(hid[par][:, :, :], act_g[par][:, :, :],
                                        U[par][:, :].rearrange("p (t s) -> p t s", t=FT), ALU.mult).then_inc(s["hid"], 1)
            b = it - 1
            if within(b, NB):
                dve.wait_ge(s["rstd"], b + 1)
                need(dve, s["xt"], b - 1)
                need(dve, s["kept"], b - 1)
                norm_tiles(nc, x, b, mv[:, 1 - par], rstd[:, 1 - par], xn[1 - par]).then_inc(s["xn"], 1)
            if within(it, NB):
                chain = Chain(dve, s["prep"], 3, it)
                stats_tiles(nc, dve, chain, x, it, stat, mv[:, par], gate).then_inc(s["mv"], 1)
                chain.close()
            b = it - 2
            if isinstance(b, int) and b == 0:
                dve.wait_ge(s["split"], 1)
                nc.vector.tensor_tensor(w_lo[:, :], w_in[:, :], w_hi[:, :].bitcast(F32), ALU.subtract).then_inc(s["split"], 1)
            if within(b, NB):
                dve.wait_ge(s["xth"], b + 1)
                need(dve, s["lg"], b - 1)
                nc.vector.tensor_tensor(xt_lo[par][:, :], XT[par][:, 0:N], xt_hi[par][:, :].bitcast(F32),
                                        ALU.subtract).then_inc(s["xtl"], 1)
        pipelined(dve, iteration, NB, DEPTH, LEAD)

    @blk.scalar
    def _(act):
        act.wait_ge(s["w_loaded"], 48)
        nc.scalar.copy(w_hi[:, :], w_in[:, :]).then_inc(s["split"], 1)

        def iteration(it, par):
            b = it - 3
            if within(b, NB):
                act.wait_ge(s["gu"], b + 1)
                need(act, s["hid"], b - 1)
                nc.scalar.activation(act_g[1 - par][:, :, :], G[1 - par][:, :].rearrange("p (t s) -> p t s", t=FT),
                                     ACT.Gelu).then_inc(s["gel"], 1)
                act.wait_ge(s["lg"], b + 1)
                nc.scalar.copy(logits[:, :, bass.ds(b, 1), :].rearrange("p t a e -> p t (a e)"),
                               L[:, 0:NH * E].rearrange("p (t e) -> p t e", t=NH)).then_inc(s["lgc"], 1)
            b = it - 1
            if within(b, NB):
                act.wait_ge(s["xt"], b + 1)
                need(act, s["lg"], b - 1)
                nc.scalar.copy(xt_hi[1 - par][:, :], XT[1 - par][:, 0:N]).then_inc(s["xth"], 1)
        pipelined(act, iteration, NB, DEPTH, LEAD)

    @blk.tensor
    def _(pe):

        def iteration(it, par):
            b = it - 3
            if isinstance(b, int) and b == 0:
                pe.wait_ge(s["d_loaded"], 32)
                pe.wait_ge(s["split"], 2)
            if within(b, NB):
                pe.wait_ge(s["xtl"], b + 1)
                need(pe, s["hid"], b - 1)
                for bank_, at in ((G[1 - par], 0), (U[1 - par], F)):
                    for t in range(FT):
                        out, cols = bank_[:, N * t:N * t + N], slice(at + 128 * t, at + 128 * t + 128)
                        nc.tensor.matmul(out, w_hi[:, cols], xt_hi[1 - par][:, :], start=True, stop=False)
                        nc.tensor.matmul(out, w_hi[:, cols], xt_lo[1 - par][:, :], start=False, stop=False)
                        last = nc.tensor.matmul(out, w_lo[:, cols], xt_hi[1 - par][:, :], start=False, stop=True)
                last.then_inc(s["gu"], 1)
                need(pe, s["lgc"], b)
                for half in range(NH):
                    out, rows, cols = L[:, E * half:E * half + E], slice(128 * half, 128 * half + 128), slice(2 * F, C)
                    nc.tensor.matmul(out, xt_hi[1 - par][:, rows], w_hi[:, cols], start=True, stop=False)
                    nc.tensor.matmul(out, xt_lo[1 - par][:, rows], w_hi[:, cols], start=False, stop=False)
                    last = nc.tensor.matmul(out, xt_hi[1 - par][:, rows], w_lo[:, cols], start=False, stop=True)
                last.then_inc(s["lg"], 1)
            b = it - 4
            if within(b, NB):
                pe.wait_ge(s["hid"], b + 1)
                need(pe, s["xadd"], b)
                for half in range(NH):
                    for t in range(FT):
                        last = nc.tensor.matmul(Y[:, D * half:D * half + D], hid[par][:, t, 128 * half:128 * half + 128],
                                                w_down[:, t, :], start=(t == 0), stop=(t == FT - 1))
                last.then_inc(s["y"], 1)
            b = it - 1
            if within(b, NB):
                pe.wait_ge(s["xn"], b + 1)
                need(pe, s["xtl"], b - 1)
                for half in range(NH):
                    last = nc.tensor.transpose(XT[1 - par][:, 128 * half:128 * half + 128], xn[1 - par][:, half, :],
                                               ident[:, :])
                last.then_inc(s["xt"], 1)
        pipelined(pe, iteration, NB, DEPTH, LEAD)


def route(nc, tag, ctx, ident, logits, weight, place, E, CAP, BG, NG):
    sb = lambda name, shape, dt=F32: ctx.enter_context(nc.sbuf_tensor(tag + name, shape, dt))
    top, low, total = sb("top", [128, NT]), sb("low", [128, NT, E]), sb("total", [128, 2, NT])
    left = [sb(f"left{n}", [128, NG, N]) for n in range(2)]
    best = [sb(f"best{n}", [128, 8]) for n in range(NG)]
    chosen, count, ones = sb("chosen", [128, NG, N]), sb("count", [128, NG, N]), sb("ones", [128, N])
    ranked = sb("ranked", [128, NG, N])
    W = [ctx.enter_context(nc.psum_tensor(tag + f"W{g}", [128, 512], F32)) for g in range(NG)]
    P = [ctx.enter_context(nc.psum_tensor(tag + f"P{g}", [128, 512], F32)) for g in range(NG)]
    s = ctx.enter_context(semaphores(nc, tag, "low exped link weighed turned back"))
    blk = ctx.enter_context(nc.Block())
    flat = lambda t: t[:, :, :, :].rearrange("p t b e -> p (t b) e")
    over = lambda ap: ap.rearrange("p (t a) -> p t a", a=1).broadcast_to([128, NT, E])

    @blk.scalar
    def _(act):
        act.wait_ge(s["low"], 1)
        nc.scalar.activation(low[:, :, :], low[:, :, :], ACT.Exp).then_inc(s["exped"], 1)

    @blk.tensor
    def _(pe):
        pe.wait_ge(s["weighed"], 1)
        for g in range(NG):
            for half in range(NH):
                tiles = weight[:, half, BG * g:BG * (g + 1), :].rearrange("p b e -> p (b e)")
                last = nc.tensor.transpose(W[g][:, 128 * half:128 * half + 128], tiles, ident[:, :])
            last.then_inc(s["turned"], 1)
        for g in range(NG):
            pe.wait_ge(s["back"], g + 1)
            for half in range(NH):
                last = nc.tensor.transpose(P[g][:, 128 * half:128 * half + 128], ranked[:, g, 128 * half:128 * half + 128],
                                           ident[:, :])
            last.then_inc(s["turned"], 1)

    @blk.vector
    def _(dve):
        done = [0]

        def link(ins):
            done[0] += 1
            ins.then_inc(s["link"], 1)
            dve.wait_ge(s["link"], done[0])

        link(nc.vector.tensor_reduce(top[:, :], flat(logits), AX.X, ALU.max))
        nc.vector.tensor_tensor(low[:, :, :], flat(logits), over(top[:, :]), ALU.subtract).then_inc(s["low"], 1)
        nc.vector.memset(ones[:, :], 1.0)
        dve.wait_ge(s["exped"], 1)
        link(nc.vector.tensor_reduce(total[:, 0, :], low[:, :, :], AX.X, ALU.add))
        link(nc.vector.reciprocal(total[:, 1, :], total[:, 0, :]))
        nc.vector.tensor_tensor(flat(weight), low[:, :, :], over(total[:, 1, :]), ALU.mult).then_inc(s["weighed"], 1)
        for g in range(NG):
            dve.wait_ge(s["turned"], g + 1)
            last = nc.vector.tensor_copy(left[0][:, g, :], W[g][:, 0:N])
        link(last)
        for r in range(CAP // 8):
            for g in range(NG):
                last = nc.vector.max(best[g][:, :], left[r % 2][:, g, :])
            link(last)
            for g in range(NG):
                last = nc.vector.match_replace(left[1 - r % 2][:, g, :], best[g][:, :], left[r % 2][:, g, :], -1.0)
            link(last)
        link(nc.vector.tensor_scalar(chosen[:, :, :], left[(CAP // 8) % 2][:, :, :], 0.0, None, ALU.is_lt))
        for g in range(NG):
            last = nc.vector.tensor_tensor_scan(count[:, g, :], ones[:, :], chosen[:, g, :], 0.0, ALU.mult, ALU.add)
        link(last)
        for g in range(NG):
            nc.vector.tensor_tensor(ranked[:, g, :], count[:, g, :], chosen[:, g, :], ALU.mult).then_inc(s["back"], 1)
        for g in range(NG):
            dve.wait_ge(s["turned"], NG + g + 1)
            for half in range(NH):
                tiles = place[:, half, BG * g:BG * (g + 1), :].rearrange("p b e -> p (b e)")
                nc.vector.tensor_copy(tiles, P[g][:, 128 * half:128 * half + 128])


def is_in_slot(nc, out, place, slot, half, b, E, CAP):
    at = place[:, half, bass.ds(b, 1), :].rearrange("p a (e b) -> p (a e) b", b=1).broadcast_to([128, E, CAP])
    all_slots = slot[:, :].rearrange("p (a c) -> p a c", a=1).broadcast_to([128, E, CAP])
    return nc.vector.tensor_tensor(out, at, all_slots, ALU.is_equal)


def gather(nc, tag, ctx, xn_all, place, slot, xg_hi, xg_lo, E, CAP):
    sb = lambda name, shape, dt=F32: ctx.enter_context(nc.sbuf_tensor(tag + name, shape, dt))
    bank = lambda name: ctx.enter_context(nc.psum_tensor(tag + name, [128, 512], F32))
    xs_hi = [sb(f"xs_hi{u}", [128, NH, D], F32R) for u in range(2)]
    xs_lo = [sb(f"xs_lo{u}", [128, NH, D], F32R) for u in range(2)]
    hot = [[sb(f"hot{u}{half}", [128, E, CAP], F32R) for half in range(NH)] for u in range(2)]
    XH, XL = ([bank(n + str(u)) for u in range(2)] for n in ("XH", "XL"))
    s = ctx.enter_context(semaphores(nc, tag, "hi lo hot got outh out0 out1"))
    blk = ctx.enter_context(nc.Block())
    DEPTH, LEAD = 2, 4

    @blk.gpsimd
    def _(pool):
        def iteration(it, par):
            if within(it, NB):
                pool.wait_ge(s["hi"], it + 1)
                need(pool, s["got"], it - 1)
                nc.gpsimd.tensor_tensor(xs_lo[par][:, :, :], xn_all[:, bass.ds(2 * it, NH), :],
                                        xs_hi[par][:, :, :].bitcast(F32), ALU.subtract).then_inc(s["lo"], 1)
        pipelined(pool, iteration, NB, DEPTH, LEAD)

    @blk.scalar
    def _(act):
        def iteration(it, par):
            if within(it, NB):
                need(act, s["got"], it - 1)
                nc.scalar.copy(xs_hi[par][:, :, :], xn_all[:, bass.ds(2 * it, NH), :]).then_inc(s["hi"], 1)
            b = it - 2
            if within(b, NB):
                act.wait_ge(s["got"], b + 1)
                nc.scalar.copy(xg_hi[:, :, bass.ds(b, 1), :].rearrange("p e a c -> p e (a c)"),
                               XH[par][:, :].rearrange("p (e c) -> p e c", c=CAP)).then_inc(s["outh"], 1)
                if par == 0:
                    nc.scalar.copy(xg_lo[:, :, bass.ds(b, 1), :].rearrange("p e a c -> p e (a c)"),
                                   XL[0][:, :].rearrange("p (e c) -> p e c", c=CAP)).then_inc(s["out0"], 2)
        pipelined(act, iteration, NB, DEPTH, LEAD)

    @blk.vector
    def _(dve):
        def iteration(it, par):
            if within(it, NB):
                need(dve, s["got"], it - 1)
                for half in range(NH):
                    last = is_in_slot(nc, hot[par][half][:, :, :], place, slot, half, it, E, CAP)
                last.then_inc(s["hot"], 1)
            b = it - 2
            if within(b, NB) and par == 1:
                dve.wait_ge(s["got"], b + 1)
                nc.vector.tensor_copy(xg_lo[:, :, bass.ds(b, 1), :].rearrange("p e a c -> p e (a c)"),
                                      XL[1][:, :].rearrange("p (e c) -> p e c", c=CAP)).then_inc(s["out1"], 2)
        pipelined(dve, iteration, NB, DEPTH, LEAD)

    @blk.tensor
    def _(pe):
        def iteration(it, par):
            if within(it, NB):
                for n in ("hot", "lo"):
                    pe.wait_ge(s[n], it + 1)
                need(pe, s["outh"], it - 1)
                need(pe, s[f"out{par}"], it - par)
                for out, xs in ((XH[par], xs_hi[par]), (XL[par], xs_lo[par])):
                    for half in range(NH):
                        last = nc.tensor.matmul(out[:, :], xs[:, half, :], hot[par][half][:, :, :],
                                                start=(half == 0), stop=(half == NH - 1))
                last.then_inc(s["got"], 1)
        pipelined(pe, iteration, NB, DEPTH, LEAD)


def experts(nc, tag, ctx, xg_hi, xg_lo, wg, wu, wd, eo_all, E, F, FT, CAP):
    S = NB * CAP
    ST = S // 128
    UNROLL = 4
    sb = lambda name, shape, dt=F32: ctx.enter_context(nc.sbuf_tensor(tag + name, shape, dt))
    bank = lambda name: ctx.enter_context(nc.psum_tensor(tag + name, [128, 512], F32))
    w_in = [sb(f"w_in{u}", [128, 2, F]) for u in range(UNROLL)]
    w_hi = [sb(f"w_hi{u}", [128, 2, F], F32R) for u in range(2)]
    w_lo = [sb(f"w_lo{u}", [128, 2, F], F32R) for u in range(2)]
    w_down = [sb(f"w_down{u}", [128, FT, D]) for u in range(UNROLL)]
    act_g = sb("act_g", [128, FT, S])
    hid = [sb(f"hid{u}", [128, FT, S]) for u in range(2)]
    eo = [sb(f"eo{u}", [128, ST, D]) for u in range(2)]
    G, U, Y = ([bank(n + str(t)) for t in range(2)] for n in ("G", "U", "Y"))
    s = ctx.enter_context(semaphores(nc, tag, "w_in0 w_in1 w_in2 w_in3 wd0 wd1 wd2 wd3 w_hi w_lo gu gel hid y eo moved0 moved1"))
    blk = ctx.enter_context(nc.Block())

    def turns(eng, iteration):
        for e in range(UNROLL):
            iteration(e, e, 0)
        with eng.Fori(1, E // UNROLL) as i:
            for u in range(UNROLL):
                iteration(UNROLL * i + u, u, i)
        iteration(E, 0, E // UNROLL)

    def half_count(e, u, i):
        return (UNROLL // 2) * i + u // 2 + 1

    @blk.sync
    def _(sp):
        def load(e, u, i):
            a, c = values(sp, e, e - 3)
            need(sp, s["w_lo"], c)
            for k, w in enumerate((wg, wu)):
                sp.dma_start(w_in[u][:, k, :], w[bass.ds(a, 1), :, :].rearrange("a p f -> p (a f)")).then_inc(s[f"w_in{u}"], 16)
            need(sp, s["y"], c)
            sp.dma_start(w_down[u][:, :, :], wd[bass.ds(a, 1), :, :].rearrange("a (t p) d -> p (a t) d", p=128)).then_inc(s[f"wd{u}"], 16)

        def move(u, i):
            for r in range(4):
                sp.dma_start(eo_all[CAP * u:CAP * u + CAP, r::4, bass.ds(i, 1), :].rearrange("p b a d -> p b (a d)"),
                             eo[u % 2][CAP * r:CAP * r + CAP, :, :]).then_inc(s[f"moved{u % 2}"], 16)

        def iteration(e, u, i):
            if not (isinstance(e, int) and e + 2 >= E):
                load(e + 2, (u + 2) % UNROLL, i + (u + 2) // UNROLL)
            if not (isinstance(e, int) and e == 0):
                v, = values(sp, e)
                sp.wait_ge(s["eo"], v)
                move((u - 1) % UNROLL, i - 1 if u == 0 else i)

        load(0, 0, 0)
        load(1, 1, 0)
        for e in range(UNROLL):
            iteration(e, e, 0)
        with sp.Fori(1, E // UNROLL - 1) as i:
            for u in range(UNROLL):
                iteration(UNROLL * i + u, u, i)
        for e in range(E - UNROLL, E):
            iteration(e, e % UNROLL, E // UNROLL - 1)
        sp.wait_ge(s["eo"], E)
        move(UNROLL - 1, E // UNROLL - 1)
        for u in range(2):
            sp.wait_ge(s[f"moved{u}"], 64 * E // 2)

    @blk.scalar
    def _(act):
        def iteration(e, u, i):
            if within(e, E):
                act.wait_ge(s[f"w_in{u}"], 32 * (i + 1))
                need(act, s["gu"], FT * (e - 1))
                nc.scalar.copy(w_hi[u % 2][:, :, :], w_in[u][:, :, :]).then_inc(s["w_hi"], 1)
            e, u = e - 1, (u - 1) % UNROLL
            if within(e, E):
                for t in range(FT):
                    act.wait_ge(s["gu"], FT * e + t + 1)
                    need(act, s["hid"], FT * (e - 1) + t + 1)
                    nc.scalar.activation(act_g[:, t, :], G[t][:, :], ACT.Gelu).then_inc(s["gel"], 1)
        turns(act, iteration)

    @blk.gpsimd
    def _(pool):
        def iteration(e, u, i):
            if within(e, E):
                pool.wait_ge(s["w_hi"], e + 1)
                nc.gpsimd.tensor_tensor(w_lo[u % 2][:, :, :], w_in[u][:, :, :], w_hi[u % 2][:, :, :].bitcast(F32),
                                        ALU.subtract).then_inc(s["w_lo"], 1)
        turns(pool, iteration)

    @blk.vector
    def _(dve):
        def down(e, u, i):
            dve.wait_ge(s["y"], e + 1)
            n = half_count(e, u, i)
            need(dve, s[f"moved{u % 2}"], 64 * (n - 1))
            nc.vector.tensor_copy(eo[u % 2][:, :, :], Y[u % 2][:, :].rearrange("p (t d) -> p t d", t=ST)).then_inc(s["eo"], 1)

        def iteration(e, u, i):
            if not (isinstance(e, int) and e == 0):
                e1, u1 = e - 1, (u - 1) % UNROLL
                for t in range(FT):
                    dve.wait_ge(s["gel"], FT * e1 + t + 1)
                    need(dve, s["y"], e1 - 1)
                    nc.vector.tensor_tensor(hid[u1 % 2][:, t, :], act_g[:, t, :], U[t][:, :], ALU.mult).then_inc(s["hid"], 1)
            if not (isinstance(e, int) and e < 2):
                u2 = (u - 2) % UNROLL
                down(e - 2, u2, i - 1 if u < 2 else i)
        turns(dve, iteration)
        down(E - 1, UNROLL - 1, E // UNROLL - 1)

    @blk.tensor
    def _(pe):
        def down(e, u, i):
            pe.wait_ge(s["hid"], FT * (e + 1))
            pe.wait_ge(s[f"wd{u}"], 16 * (i + 1))
            need(pe, s["eo"], e - 1)
            for st in range(ST):
                for t in range(FT):
                    last = nc.tensor.matmul(Y[u % 2][:, D * st:D * st + D], hid[u % 2][:, t, 128 * st:128 * st + 128],
                                            w_down[u][:, t, :], start=(t == 0), stop=(t == FT - 1))
            last.then_inc(s["y"], 1)

        def iteration(e, u, i):
            if within(e, E):
                pe.wait_ge(s["w_lo"], e + 1)
                hi = xg_hi[:, bass.ds(e, 1), :, :].rearrange("p a b c -> p (a b c)")
                lo = xg_lo[:, bass.ds(e, 1), :, :].rearrange("p a b c -> p (a b c)")
                for t in range(FT):
                    need(pe, s["hid"], FT * (e - 1) + t + 1)
                    for k, bank_ in enumerate((G[t], U[t])):
                        cols = slice(128 * t, 128 * t + 128)
                        nc.tensor.matmul(bank_[:, :], w_hi[u % 2][:, k, cols], hi, start=True, stop=False)
                        nc.tensor.matmul(bank_[:, :], w_hi[u % 2][:, k, cols], lo, start=False, stop=False)
                        last = nc.tensor.matmul(bank_[:, :], w_lo[u % 2][:, k, cols], hi, start=False, stop=True)
                    last.then_inc(s["gu"], 1)
            if not (isinstance(e, int) and e == 0):
                down(e - 1, (u - 1) % UNROLL, i - 1 if u == 0 else i)
        turns(pe, iteration)


def combine(nc, tag, ctx, x, ident, place, weight, slot, eo_all, E, CAP, NJ):
    sb = lambda name, shape, dt=F32: ctx.enter_context(nc.sbuf_tensor(tag + name, shape, dt))
    bank = lambda name: ctx.enter_context(nc.psum_tensor(tag + name, [128, 512], F32))
    hot = [sb(f"hot{u}", [128, NH, E, CAP]) for u in range(2)]
    mix = [sb(f"mix{u}", [128, NH, E, CAP]) for u in range(2)]
    mix_t = [sb(f"mix_t{u}", [128, NJ, N]) for u in range(2)]
    T = [[bank(f"T{u}{k}") for k in range(2)] for u in range(2)]
    Y = [bank(f"Y{u}") for u in range(2)]
    s = ctx.enter_context(semaphores(nc, tag, "hot mix t0 t1 ta tv y xadd"))
    blk = ctx.enter_context(nc.Block())
    DEPTH, LEAD = 4, 6

    @blk.gpsimd
    def _(pool):
        def iteration(it, par):
            if within(it, NB):
                pool.wait_ge(s["hot"], it + 1)
                need(pool, s["t1"], it - 1)
                w = weight[:, :, bass.ds(it, 1), :].rearrange("p t a e -> p t e a").broadcast_to([128, NH, E, CAP])
                nc.gpsimd.tensor_tensor(mix[par][:, :, :, :], hot[par][:, :, :, :], w, ALU.mult).then_inc(s["mix"], 1)
        pipelined(pool, iteration, NB, DEPTH, LEAD)

    @blk.vector
    def _(dve):
        def iteration(it, par):
            if within(it, NB):
                need(dve, s["mix"], it - 1)
                for half in range(NH):
                    last = is_in_slot(nc, hot[par][:, half, :, :], place, slot, half, it, E, CAP)
                last.then_inc(s["hot"], 1)
            b = it - 2
            if within(b, NB):
                dve.wait_ge(s["t1"], b + 1)
                need(dve, s["y"], b - 1)
                nc.vector.tensor_copy(mix_t[par][:, 2:4, :], T[par][1][:, :].rearrange("p (j s) -> p j s", j=2)).then_inc(s["tv"], 1)
            b = it - 4
            if within(b, NB):
                dve.wait_ge(s["y"], b + 1)
                nc.vector.tensor_tensor(x[:, bass.ds(2 * b, NH), :], x[:, bass.ds(2 * b, NH), :],
                                        Y[par][:, 0:N].rearrange("p (t d) -> p t d", t=NH), ALU.add).then_inc(s["xadd"], 1)
        pipelined(dve, iteration, NB, DEPTH, LEAD)

    @blk.scalar
    def _(act):
        def iteration(it, par):
            b = it - 2
            if within(b, NB):
                act.wait_ge(s["t0"], b + 1)
                need(act, s["y"], b - 1)
                nc.scalar.copy(mix_t[par][:, 0:2, :], T[par][0][:, :].rearrange("p (j s) -> p j s", j=2)).then_inc(s["ta"], 1)
        pipelined(act, iteration, NB, DEPTH, LEAD)

    @blk.tensor
    def _(pe):
        def iteration(it, par):
            b = it - 1
            if within(b, NB):
                pe.wait_ge(s["mix"], b + 1)
                for k, (freed, signal) in enumerate((("ta", "t0"), ("tv", "t1"))):
                    need(pe, s[freed], b - 1)
                    for j in range(2 * k, 2 * k + 2):
                        for half in range(NH):
                            at = N * (j % 2) + 128 * half
                            last = nc.tensor.transpose(
                                T[1 - par][k][:, at:at + 128],
                                mix[1 - par][:, half, 4 * j:4 * j + 4, :].rearrange("p e c -> p (e c)"), ident[:, :])
                    last.then_inc(s[signal], 1)
            b = it - 3
            if within(b, NB):
                pe.wait_ge(s["ta"], b + 1)
                pe.wait_ge(s["tv"], b + 1)
                need(pe, s["xadd"], b - 1)
                for half in range(NH):
                    for j in range(NJ):
                        rows = eo_all[:, bass.ds(b, 1), j, :].rearrange("p a d -> p (a d)")
                        last = nc.tensor.matmul(Y[1 - par][:, D * half:D * half + D],
                                                mix_t[1 - par][:, j, 128 * half:128 * half + 128], rows,
                                                start=(j == 0), stop=(j == NJ - 1))
                last.then_inc(s["y"], 1)
        pipelined(pe, iteration, NB, DEPTH, LEAD)


def rotary_attention(nc, ctx, x, ident, wqk, wv, wout, bout, cos, sin):
    H, DH = 16, 64
    PAIRS = H // 2
    W = 2 * N
    LT, LS, LP, LO = 2, 5, 5, 6

    def sb(name, shape, dt=F32):
        return ctx.enter_context(nc.sbuf_tensor("b_" + name, shape, dt))

    def bank(name):
        return ctx.enter_context(nc.psum_tensor("b_" + name, [128, 512], F32))

    CW = 3 * H * DH
    VC = 2 * H * DH
    w_in, w_hi, w_lo = sb("w_in", [128, CW]), sb("w_hi", [128, CW], F32R), sb("w_lo", [128, CW], F32R)
    w_out = sb("w_out", [128, PAIRS, D])
    b_all = sb("b_all", [128, D])
    turn_c, turn_s = sb("turn_c", [128, W]), sb("turn_s", [128, W])
    stat, mv, rstd = sb("stat", [128, NH, 6]), sb("mv", [128, NH, 2]), sb("rstd", [128, 2, NH])
    gate, consts, ones = sb("gate", [128, 1]), sb("consts", [128, 2]), sb("ones", [128, 1, 1, 1])
    xn = sb("xn", [128, NH, D])
    xt_hi, xt_lo = sb("xt_hi", [128, N], F32R), sb("xt_lo", [128, N], F32R)
    swapped = [sb(f"swapped{u}", [128, W]) for u in range(2)]
    scaled = [sb(f"scaled{u}", [128, W]) for u in range(2)]
    turned = sb("turned", [128, W])
    qk = [sb(f"qk{u}", [128, W]) for u in range(2)]
    qk_hi, qk_lo = sb("qk_hi", [128, PAIRS, W], F32R), sb("qk_lo", [128, PAIRS, W], F32R)
    v = [sb(f"v{u}", [128, NH, H * DH]) for u in range(2)]
    prob = [sb(f"prob{n}", [128, 2, N]) for n in range(4)]
    prob_t = [sb(f"prob_t{n}", [128, 2, N]) for n in range(4)]
    shift, total, r_sum = sb("shift", [128, 4, 2]), sb("total", [128, 4, 2]), sb("r_sum", [128, 4, 2])
    r_wide = [sb(f"r_wide{u}", [128, NH, 2, DH]) for u in range(2)]
    r_t = sb("r_t", [128, N])
    o_t = sb("o_t", [128, PAIRS, N])
    S, PT = [bank("S0"), bank("S1")], [bank("PT0"), bank("PT1")]
    OT, M, QK, VY = bank("OT"), bank("M"), bank("QK"), bank("VY")
    names = ("w_loaded c_loaded hi split ready prep mv veps rstd xn xb xt xth xtl qkp sw tu qk qh ql vp vs "
             "sc mx ex tr pt rc rw nt nts ot o y xadd")
    s = ctx.enter_context(semaphores(nc, "b_", names))
    LOOPS = (NB - 2) // 2
    DRAIN = 10

    def stepper(eng, iteration):
        iteration(0, 0, True, True)
        with eng.Fori(0, LOOPS) as i:
            for u in range(2):
                iteration(2 * i + 1 + u, (1 + u) % 2, True, True)
        iteration(NB - 1, (NB - 1) % 2, True, False)
        iteration(NB, NB % 2, False, False)

    def lagged(b, step, lag):
        return (b, step - lag) if step >= lag else (b - 1, step - lag + H)

    def due(b, step, lag, attend):
        n, h = lagged(b, step, lag)
        return (n, h) if (not isinstance(n, int) or n >= 0) and (attend or step < lag) else None

    def projected(b, step, lag, prep):
        at = step - lag
        if at % 2 == 0:
            return None
        if at < 5:
            return (b, PAIRS - 2 + at // 2) if within(b, NB) and not (at < 0 and isinstance(b, int) and b == 0) else None
        return (b + 1, at // 2 - 2) if prep else None

    LR, LH = 1, 3
    X_STEP = 4
    V_STEPS = (8, 10, 12, 14)
    Y_STEP = 6
    blk = ctx.enter_context(nc.Block())

    @blk.sync
    def _(sp):
        sp.dma_start(w_in[:, 0:VC], wqk).then_inc(s["w_loaded"], 16)
        sp.dma_start(w_in[:, VC:CW], wv).then_inc(s["w_loaded"], 16)
        sp.dma_start(turn_c[:, :], cos).then_inc(s["c_loaded"], 16)
        sp.dma_start(turn_s[:, :], sin).then_inc(s["c_loaded"], 16)
        sp.dma_start(w_out[:, :, :], wout.rearrange("(t p) d -> p t d", p=128)).then_inc(s["c_loaded"], 16)
        sp.dma_start(b_all[:, :], bout.rearrange("(a d) -> a d", a=1).broadcast_to([128, D])).then_inc(s["c_loaded"], 16)

    @blk.gpsimd
    def _(pool):
        nc.gpsimd.memset(consts[:, 0:1], EPS)
        nc.gpsimd.memset(consts[:, 1:2], -0.5)
        nc.gpsimd.memset(ones[:, :, :, :], 1.0).then_inc(s["ready"], 1)
        pool.wait_ge(s["ready"], 1)
        pool.wait_ge(s["c_loaded"], 64)

        def prep_r(b):
            pool.wait_ge(s["mv"], b + 1)
            rstd_tiles(nc, pool, mv, consts, rstd, s["veps"], b + 1).then_inc(s["rstd"], 1)

        def prep_x(b):
            pool.wait_ge(s["xn"], b + 1)
            nc.gpsimd.tensor_tensor(x[:, bass.ds(2 * b, 2), :], x[:, bass.ds(2 * b, 2), :],
                                    b_all[:, :].rearrange("p (a d) -> p a d", a=1).broadcast_to([128, NH, D]),
                                    ALU.add).then_inc(s["xb"], 1)

        def rotate(b, p):
            pool.wait_ge(s["sw"], PAIRS * b + p + 1)
            need(pool, s["qk"], PAIRS * b + p)
            nc.gpsimd.tensor_tensor(turned[:, :], swapped[p % 2][:, :], turn_s[:, :], ALU.mult).then_inc(s["tu"], 1)
            pool.wait_ge(s["tu"], PAIRS * b + p + 1)
            need(pool, s["ql"], PAIRS * b + p - 1)
            nc.gpsimd.tensor_tensor(qk[p % 2][:, :], scaled[p % 2][:, :], turned[:, :], ALU.add).then_inc(s["qk"], 1)

        def widen(b, h):
            pool.wait_ge(s["rc"], H * b + h + 1)
            need(pool, s["nt"], PAIRS * b + h // 2 - 1)
            two = r_sum[:, h % 4 - 1:h % 4 + 1, :].rearrange("p h (t a) -> p t h a", a=1)
            nc.gpsimd.tensor_tensor(r_wide[(h // 2) % 2][:, :, :, :], two.broadcast_to([128, NH, 2, DH]),
                                    ones[:, :, :, :].broadcast_to([128, NH, 2, DH]), ALU.mult).then_inc(s["rw"], 1)

        prep_r(0)
        prep_x(0)
        for p in range(PAIRS - 2):
            rotate(0, p)

        def iteration(b, par, attend, prep):
            for step in range(H if attend else DRAIN):
                if (nh := due(b, step, LT, attend)) is not None and nh[1] % 2:
                    widen(*nh)
                if (pq := projected(b, step, LR, prep)) is not None:
                    rotate(*pq)
                if prep and step == 0:
                    prep_r(b + 1)
                if prep and step == 2:
                    prep_x(b + 1)
        stepper(pool, iteration)

    @blk.tensor
    def _(pe):
        pe.wait_ge(s["c_loaded"], 64)
        pe.wait_ge(s["split"], 1)

        def transpose_x(b):
            pe.wait_ge(s["xn"], b + 1)
            need(pe, s["sw"], PAIRS * b)
            for half in range(NH):
                last = nc.tensor.transpose(QK[:, 128 * half:128 * half + 128], xn[:, half, :], ident[:, :])
            last.then_inc(s["xt"], 1)

        def project(b, p, bank=QK, banks=1):
            pe.wait_ge(s["xtl"], b + 1)
            need(pe, s["sw"], PAIRS * b + p + 1 - banks)
            for k in range(2):
                out, cols = bank[:, N * k:N * k + N], slice(128 * (2 * p + k), 128 * (2 * p + k) + 128)
                nc.tensor.matmul(out, w_hi[:, cols], xt_hi[:, :], start=True, stop=False)
                nc.tensor.matmul(out, w_hi[:, cols], xt_lo[:, :], start=False, stop=False)
                last = nc.tensor.matmul(out, w_lo[:, cols], xt_hi[:, :], start=False, stop=True)
            last.then_inc(s["qkp"], 1)

        def project_v(b, c):
            pe.wait_ge(s["xtl"], b + 1)
            need(pe, s["vs"], 4 * b + c)
            if c == 0:
                need(pe, s["xadd"], b - 1)
            rows = slice(128 * (c // 2), 128 * (c // 2) + 128)
            cols = slice(VC + 512 * (c % 2), VC + 512 * (c % 2) + 512)
            nc.tensor.matmul(VY[:, :], xt_hi[:, rows], w_hi[:, cols], start=True, stop=False)
            nc.tensor.matmul(VY[:, :], xt_lo[:, rows], w_hi[:, cols], start=False, stop=False)
            nc.tensor.matmul(VY[:, :], xt_hi[:, rows], w_lo[:, cols], start=False, stop=True).then_inc(s["vp"], 1)

        def scores(b, h):
            pe.wait_ge(s["ql"], PAIRS * b + h // 2 + 1)
            need(pe, s["ex"], H * b + h - 1)
            rows = slice(DH * (h % 2), DH * (h % 2) + DH)
            for t in range(NH):
                out, q, k = S[h % 2][:, N * t:N * t + N], slice(128 * t, 128 * t + 128), slice(N, W)
                nc.tensor.matmul(out, qk_hi[rows, h // 2, q], qk_hi[rows, h // 2, k], start=True, stop=False)
                nc.tensor.matmul(out, qk_hi[rows, h // 2, q], qk_lo[rows, h // 2, k], start=False, stop=False)
                last = nc.tensor.matmul(out, qk_lo[rows, h // 2, q], qk_hi[rows, h // 2, k], start=False, stop=True)
            last.then_inc(s["sc"], 1)

        def transpose_p(b, h):
            pe.wait_ge(s["ex"], H * b + h + 1)
            need(pe, s["pt"], H * b + h - 1)
            for t in range(NH):
                for kt in range(NH):
                    last = nc.tensor.transpose(PT[h % 2][:, N * kt + 128 * t:N * kt + 128 * t + 128],
                                               prob[h % 4][:, t, 128 * kt:128 * kt + 128], ident[:, :])
            last.then_inc(s["tr"], 1)

        def attend_v(b, par, p):
            pe.wait_ge(s["pt"], H * b + 2 * p + 2)
            if p == 0:
                pe.wait_ge(s["vs"], 4 * (b + 1))
            need(pe, s["o"], PAIRS * b + p)
            for kt in range(NH):
                for g in range(2):
                    h = 2 * p + g
                    last = nc.tensor.matmul(OT[DH * g:DH * g + DH, 0:N], v[par][:, kt, DH * h:DH * h + DH],
                                            prob_t[h % 4][:, kt, :], start=(kt == 0), stop=(kt == NH - 1))
            last.then_inc(s["ot"], 1)

        def turn_sums(b, p):
            pe.wait_ge(s["rw"], PAIRS * b + p + 1)
            need(pe, s["nts"], PAIRS * b + p)
            for t in range(NH):
                last = nc.tensor.transpose(M[:, 128 * t:128 * t + 128],
                                           r_wide[p % 2][:, t, :, :].rearrange("p h d -> p (h d)"), ident[:, :])
            last.then_inc(s["nt"], 1)

        def project_out(b):
            pe.wait_ge(s["o"], PAIRS * (b + 1))
            pe.wait_ge(s["vs"], 4 * min(b + 2, NB) if isinstance(b, int) else 4 * (b + 2))
            for half in range(NH):
                for p in range(PAIRS):
                    last = nc.tensor.matmul(VY[:, D * half:D * half + D], o_t[:, p, 128 * half:128 * half + 128],
                                            w_out[:, p, :], start=(p == 0), stop=(p == PAIRS - 1))
            last.then_inc(s["y"], 1)

        transpose_x(0)
        for p in range(PAIRS - 2):
            project(0, p, (QK, M)[p % 2], 2)
        for c in range(4):
            project_v(0, c)

        def iteration(b, par, attend, prep):
            for step in range(H if attend else DRAIN):
                if attend:
                    scores(b, step)
                if (nh := due(b, step, LT, attend)) is not None:
                    transpose_p(*nh)
                if (nh := due(b, step, LP, attend)) is not None and nh[1] % 2:
                    attend_v(nh[0], par if step >= LP else 1 - par, nh[1] // 2)
                if (nh := due(b, step, LS, attend)) is not None and nh[1] % 2:
                    turn_sums(nh[0], nh[1] // 2)
                if step == Y_STEP and not (isinstance(b, int) and b == 0):
                    project_out(b - 1)
                if step == X_STEP and prep:
                    transpose_x(b + 1)
                if (pq := projected(b, step, 0, prep)) is not None:
                    project(*pq)
                if step in V_STEPS and prep:
                    project_v(b + 1, V_STEPS.index(step))
        stepper(pe, iteration)

    @blk.scalar
    def _(act):
        act.wait_ge(s["w_loaded"], 32)
        nc.scalar.copy(w_hi[:, :], w_in[:, :]).then_inc(s["hi"], 1)

        def prep_t(b):
            act.wait_ge(s["xt"], b + 1)
            need(act, s["qkp"], PAIRS * b)
            need(act, s["vp"], 4 * b)
            nc.scalar.copy(xt_hi[:, :], QK[:, 0:N]).then_inc(s["xth"], 1)

        def copy_v(b, par, c):
            act.wait_ge(s["vp"], 4 * b + c + 1)
            need(act, s["ot"], PAIRS * (b - 1))
            nc.scalar.copy(v[par][:, c // 2, 512 * (c % 2):512 * (c % 2) + 512], VY[:, :]).then_inc(s["vs"], 1)

        def exps(b, h):
            act.wait_ge(s["mx"], H * b + h + 1)
            need(act, s["tr"], H * b + h - 3)
            for t in range(NH):
                last = nc.scalar.activation(prob[h % 4][:, t, :], S[h % 2][:, N * t:N * t + N], ACT.Exp,
                                            bias=shift[:, h % 4, t:t + 1], accum_out=total[:, h % 4, t:t + 1])
            last.then_inc(s["ex"], 1)

        def copy_p(b, h):
            act.wait_ge(s["tr"], H * b + h + 1)
            need(act, s["ot"], PAIRS * b + h // 2 - 1)
            nc.scalar.copy(prob_t[h % 4][:, :, :], PT[h % 2][:, :].rearrange("p (k q) -> p k q", k=NH)).then_inc(s["pt"], 1)

        def copy_sums(b, p):
            act.wait_ge(s["nt"], PAIRS * b + p + 1)
            need(act, s["o"], PAIRS * b + p)
            nc.scalar.copy(r_t[:, :], M[:, 0:N]).then_inc(s["nts"], 1)

        def split_hi(b, p):
            act.wait_ge(s["qk"], PAIRS * b + p + 1)
            need(act, s["sc"], H * (b - 1) + 2 * p + 2)
            nc.scalar.copy(qk_hi[:, p, :], qk[p % 2][:, :]).then_inc(s["qh"], 1)

        prep_t(0)
        for p in range(PAIRS - 2):
            split_hi(0, p)
        for c in range(4):
            copy_v(0, 0, c)

        def iteration(b, par, attend, prep):
            for step in range(H if attend else DRAIN):
                if step == X_STEP + 1 and prep:
                    prep_t(b + 1)
                if (pq := projected(b, step, LH, prep)) is not None:
                    split_hi(*pq)
                if attend:
                    exps(b, step)
                if (nh := due(b, step, LT, attend)) is not None:
                    copy_p(*nh)
                if (nh := due(b, step, LS, attend)) is not None and nh[1] % 2:
                    copy_sums(nh[0], nh[1] // 2)
                if step in V_STEPS and prep:
                    copy_v(b + 1, 1 - par, V_STEPS.index(step))
        stepper(act, iteration)

    @blk.vector
    def _(dve):
        dve.wait_ge(s["hi"], 1)
        nc.vector.tensor_tensor(w_lo[:, :], w_in[:, :], w_hi[:, :].bitcast(F32), ALU.subtract).then_inc(s["split"], 1)
        dve.wait_ge(s["c_loaded"], 64)

        def prep_a(b):
            chain = Chain(dve, s["prep"], 3, b)
            need(dve, s["xb"], b)
            stats_tiles(nc, dve, chain, x, b, stat, mv, gate).then_inc(s["mv"], 1)
            chain.close()

        def prep_n(b):
            dve.wait_ge(s["rstd"], b + 1)
            need(dve, s["xt"], b)
            norm_tiles(nc, x, b, mv, rstd, xn).then_inc(s["xn"], 1)

        def prep_b(b):
            dve.wait_ge(s["xth"], b + 1)
            nc.vector.tensor_tensor(xt_lo[:, :], QK[:, 0:N], xt_hi[:, :].bitcast(F32), ALU.subtract).then_inc(s["xtl"], 1)

        def rotate(b, p, bank=QK):
            dve.wait_ge(s["qkp"], PAIRS * b + p + 1)
            need(dve, s["qk"], PAIRS * b + p - 1)
            nc.vector.tensor_tensor(scaled[p % 2][:, :], bank[:, :], turn_c[:, :], ALU.mult)
            nc.vector.stream_shuffle(swapped[p % 2][:, :], bank[:, :], [i ^ 1 for i in range(32)]).then_inc(s["sw"], 1)

        def split_lo(b, p):
            dve.wait_ge(s["qh"], PAIRS * b + p + 1)
            nc.vector.tensor_tensor(qk_lo[:, p, :], qk[p % 2][:, :], qk_hi[:, p, :].bitcast(F32),
                                    ALU.subtract).then_inc(s["ql"], 1)

        def greatest(b, h):
            dve.wait_ge(s["sc"], H * b + h + 1)
            need(dve, s["ex"], H * b + h - 3)
            nc.vector.tensor_reduce(shift[:, h % 4, :], S[h % 2][:, :].rearrange("p (t k) -> p t k", t=NH), AX.X,
                                    ALU.max, negate=True).then_inc(s["mx"], 1)

        def inverse(b, h):
            dve.wait_ge(s["ex"], H * b + h + 1)
            need(dve, s["rw"], PAIRS * b + h // 2 - 1)
            nc.vector.reciprocal(r_sum[:, h % 4, :], total[:, h % 4, :]).then_inc(s["rc"], 1)

        def normalise(b, p):
            dve.wait_ge(s["ot"], PAIRS * b + p + 1)
            dve.wait_ge(s["nts"], PAIRS * b + p + 1)
            if p == 0:
                need(dve, s["y"], b)
            nc.vector.tensor_tensor(o_t[:, p, :], OT[:, 0:N], r_t[:, :], ALU.mult).then_inc(s["o"], 1)

        prep_a(0)
        prep_n(0)
        prep_b(0)
        for p in range(PAIRS - 2):
            rotate(0, p, (QK, M)[p % 2])
            if p:
                split_lo(0, p - 1)
        split_lo(0, PAIRS - 3)

        def iteration(b, par, attend, prep):
            for step in range(H if attend else DRAIN):
                if attend:
                    greatest(b, step)
                if step == Y_STEP + 1 and not (isinstance(b, int) and b == 0):
                    dve.wait_ge(s["y"], b)
                    dve.wait_ge(s["xb"], b)
                    tiles = bass.ds(2 * (b - 1), 2)
                    nc.vector.tensor_tensor(x[:, tiles, :], x[:, tiles, :], VY[:, 0:N].rearrange("p (t d) -> p t d", t=NH),
                                            ALU.add).then_inc(s["xadd"], 1)
                if step == X_STEP + 1 and prep:
                    prep_b(b + 1)
                if (pq := projected(b, step, LR, prep)) is not None:
                    rotate(*pq)
                if (nh := due(b, step, LT, attend)) is not None:
                    inverse(*nh)
                if (nh := due(b, step, LO, attend)) is not None and nh[1] % 2:
                    normalise(nh[0], nh[1] // 2)
                if (pq := projected(b, step, LH, prep)) is not None:
                    split_lo(*pq)
                if prep and step == 0:
                    prep_a(b + 1)
                if prep and step == 2:
                    prep_n(b + 1)
        stepper(dve, iteration)


def distance_buckets():
    hot = np.zeros((33, 384), np.float32)
    for u in range(384):
        n = 127 - u + 128
        if n < 0:
            hot[32, u] = 1.0
        elif n < 16:
            hot[n, u] = 1.0
        else:
            hot[min(16 + int(math.log(n / 16) / math.log(8) * 16 + 1e-9), 31), u] = 1.0
    return hot


def load_constants(nc, x, x_in, ident, ident_in, with_x):
    with nc.semaphore("ident_loaded") as loaded, nc.Block() as blk:
        @blk.sync
        def _(sp):
            sp.dma_start(ident[:, :], ident_in).then_inc(loaded, 16)
            if with_x:
                sp.dma_start(x[:, :, :], x_in.rearrange("b (t p) d -> p (b t) d", p=128)).then_inc(loaded, 16)
            sp.wait_ge(loaded, 32 if with_x else 16)


def store(nc, x, out):
    with nc.semaphore("stored") as stored, nc.Block() as blk:
        @blk.sync
        def _(sp):
            sp.dma_start(out.rearrange("b (t p) d -> p (b t) d", p=128), x[:, :, :]).then_inc(stored, 16)
            sp.wait_ge(stored, 16)


def build(nc, t, out, parts=("a", "f1", "b", "f2")):
    with ExitStack() as top:
        x = top.enter_context(nc.sbuf_tensor("tokens", [128, NT, D], F32))
        ident = top.enter_context(nc.sbuf_tensor("identity", [128, 128], F32))
        load_constants(nc, x, t["x"], ident, t["ident"], parts[0] != "a")
        for part in parts:
            if part == "a":
                with ExitStack() as ctx:
                    causal_attention(nc, ctx, x, ident, t["x"], t["a_wq"], t["a_wk"], t["a_wv"], t["a_wo"], t["a_bo"],
                                     t["rel_emb"], t["buckets"])
            elif part == "b":
                with ExitStack() as ctx:
                    rotary_attention(nc, ctx, x, ident, t["b_wqk"], t["b_wv"], t["b_wout"], t["b_bout"], t["cos"], t["sin"])
            else:
                expert_choice_ffn(nc, part + "_", x, ident, t["gate_w"], t["wg"], t["wu"], t["wd"], t["ws_g"], t["ws_u"],
                                  t["ws_d"], t["slots"])
        store(nc, x, out)


def rotation():
    angle = (np.arange(N, dtype=np.float32)[:, None] *
             (np.float32(1.0) / np.float32(10000.0) ** (np.arange(0, 32, 2, dtype=np.float32) / np.float32(32)))[None, :])
    cos, sin = np.ones((2, 64, N), np.float32), np.zeros((2, 64, N), np.float32)
    for d in range(32):
        cos[:, d] = np.cos(angle[:, d // 2])
        sin[:, d] = np.sin(angle[:, d // 2]) * (1 if d % 2 else -1)
    cos, sin = cos.reshape(128, N), sin.reshape(128, N)
    scale = np.float32(64 ** -0.5)
    return np.concatenate([cos * scale, cos], 1), np.concatenate([sin * scale, sin], 1)


def constants():
    cos, sin = rotation()
    return {"ident": np.eye(128, dtype=np.float32), "buckets": distance_buckets(), "cos": cos, "sin": sin,
            "slots": np.arange(1, 33, dtype=np.float32)}


def laid_out(i):
    A, B, Fn = "L0_attn_a_", "L0_attn_b_", "L0_ffn_"
    swap = lambda a: np.ascontiguousarray(np.swapaxes(a, -1, -2))
    wq, wk, wv = i[B + "Wq"], i[B + "Wkv"][:, :1024], i[B + "Wkv"][:, 1024:]
    wqk = np.stack([wq.reshape(D, 8, 128), wk.reshape(D, 8, 128)], 2).reshape(D, 2048)
    return {"b_wqk": wqk, "b_wv": np.ascontiguousarray(wv), "b_wout": i[B + "Wout"], "b_bout": i[B + "bout"],
            "x": i[A + "x"], "a_wq": i[A + "Wq"], "a_wk": i[A + "Wk"], "a_wv": i[A + "Wv"], "a_wo": i[A + "Wo"],
            "a_bo": i[A + "bo"], "rel_emb": i[A + "rel_emb"],
            "gate_w": swap(i[Fn + "gate_w"]), "wg": swap(i[Fn + "Wg"]), "wu": swap(i[Fn + "Wu"]), "wd": swap(i[Fn + "Wd"]),
            "ws_g": swap(i[Fn + "Ws_g"]), "ws_u": swap(i[Fn + "Ws_u"]), "ws_d": swap(i[Fn + "Ws_d"])}


def kernel(**inputs):
    from concourse import bacc
    from concourse.bass_utils import run_bass_kernel_spmd

    nc = bacc.Bacc("TRN2", target_bir_lowering=False, num_devices=1)
    arrays = {n: np.ascontiguousarray(a) for n, a in {**laid_out(inputs), **constants()}.items()}
    tensors = {n: nc.dram_tensor(n, a.shape, mybir.dt.from_np(a.dtype), kind="ExternalInput").ap()
               for n, a in arrays.items()}
    out = nc.dram_tensor("out", (NB, N, D), F32, kind="ExternalOutput").ap()
    build(nc, tensors, out)
    return run_bass_kernel_spmd(nc, [arrays], core_ids=[0]).results[0]["out"]
```

```python
import math
from contextlib import ExitStack, contextmanager

import numpy as np
import concourse.bass as bass
from concourse import mybir

F32 = mybir.dt.float32
F32R = mybir.dt.float32r
BF16 = mybir.dt.bfloat16
ALU = mybir.AluOpType
ACT = mybir.ActivationFunctionType
AX = mybir.AxisListType

NB = 16
N = 256
D = 128
NH = 2
NT = NB * NH
EPS = 1e-5
BIG = 1.0e38


@contextmanager
def semaphores(nc, tag, names):
    held = {n: nc.alloc_semaphore(tag + n) for n in names.split()}
    yield held
    nc.clear_and_free_semaphores(list(held.values()))
    nc.all_engine_barrier()


def need(eng, sem, value):
    if isinstance(value, int) and value <= 0:
        return
    eng.wait_ge(sem, value)


def values(eng, *terms):
    return [t if isinstance(t, int) else eng.snap(t) for t in terms]


def stats_tiles(nc, dve, chain, x, b, stat, mv, gate):
    for half in range(NH):
        chain.link(nc.vector.bn_stats(stat[:, half, :], x[:, 2 * b + half, :]))
    chain.reach()
    chain.link(nc.vector.memset(gate[:, :], 0.0))
    for half in range(NH):
        last = nc.vector.bn_aggr(mv[:, half, :], stat[:, half, :])
    return last


def rstd_tiles(nc, pool, mv, consts, rstd, added, count):
    two = lambda c: consts[:, c:c + 1].broadcast_to([128, NH])
    nc.gpsimd.tensor_tensor(rstd[:, 0, :], mv[:, :, 1], two(0), ALU.add).then_inc(added, 1)
    pool.wait_ge(added, count)
    return nc.gpsimd.tensor_tensor(rstd[:, 1, :], rstd[:, 0, :], two(1), ALU.pow)


def norm_tiles(nc, x, b, mv, rstd, xn):
    for half in range(NH):
        last = nc.vector.tensor_scalar(xn[:, half, :], x[:, 2 * b + half, :], mv[:, half, 0:1],
                                       rstd[:, 1, half:half + 1], ALU.subtract, ALU.mult)
    return last


class Chain:

    def __init__(self, eng, sem, links, batch):
        self.eng, self.sem, self.links, self.base, self.n = eng, sem, links, batch * links, 0

    def link(self, ins):
        self.n += 1
        ins.then_inc(self.sem, 1)

    def reach(self, n=None):
        self.eng.wait_ge(self.sem, self.base + (self.n if n is None else n))

    def close(self):
        assert self.n == self.links, (self.n, self.links)


def causal_attention(nc, ctx, x, ident, x_in, wq, wk, wv, wo, bo, rel_emb, buckets):
    H, DH = 16, 8
    GROUPS, GH = 4, 4
    SCALE = DH ** -0.5
    LT, LP, LN_ = 3, 6, 8
    PARTS = [(0, 2), (1, 1), (2, 0), (0, 1), (1, 0), (0, 0)]
    RUNS = [(5, 1), (3, 2), (0, 3)]
    place_of = lambda side, p: p if side == 0 else 2 - p
    KR = DH * len(PARTS)

    def sb(name, shape, dt=F32):
        return ctx.enter_context(nc.sbuf_tensor("a_" + name, shape, dt))

    def bank(name):
        return ctx.enter_context(nc.psum_tensor("a_" + name, [128, 512], F32))

    w_in = sb("w_in", [128, 4, D])
    w_hi, w_lo = sb("w_hi", [128, 3, D], F32R), sb("w_lo", [128, 3, D], F32R)
    bo_all = sb("bo_all", [128, D])
    rel = sb("rel", [64, H])
    hot = sb("hot", [64, 384])
    dist_bias = sb("dist_bias", [H, 384])
    bias = sb("bias", [128, H, 256])
    stat, mv, rstd = sb("stat", [128, NT, 6]), sb("mv", [128, NT, 2]), sb("rstd", [128, 2, NT])
    gate, gate2, consts = sb("gate", [128, 1]), sb("gate2", [1, 5]), sb("consts", [128, 2])
    xn = sb("xn", [128, NH, D])
    xt_hi, xt_lo = sb("xt_hi", [128, N], F32R), sb("xt_lo", [128, N], F32R)
    part = [sb(f"part{n}", [128, 2 * N], BF16) for n in range(3)]
    rest = sb("rest", [128, 2 * N])
    qk_pack = [[sb(f"pack{s}{u}", [KR, H, N], BF16) for u in range(2)] for s in range(2)]
    v_pad = [sb(f"v_pad{u}", [128, NH, H, 32]) for u in range(2)]
    prob = [sb(f"prob{n}", [128, 384]) for n in range(4)]
    shift = sb("shift", [128, 4, 2])
    prob_t = [sb(f"prob_t{n}", [128, 384]) for n in range(8)]
    o_t = sb("o_t", [128, N])
    r_sum = sb("r_sum", [128, NH, GH])
    o = sb("o", [128, NH, D])
    of_t = sb("of_t", [128, N])
    parts = nc.dram_tensor("a_parts", (2, 2, 3, DH, H, N), BF16)
    SKEW = 8
    scratch = nc.dram_tensor("a_bias_by_distance", (SKEW, H, 384), F32)

    S, PT = [bank("S0"), bank("S1")], [bank("PT0"), bank("PT1")]
    OT, ON, QK, M = bank("OT"), bank("ON"), bank("QK"), bank("M")

    names = ("w_loaded rel_loaded hot_loaded x0_loaded x_loaded bo_loaded w_split dist_done dist_copied dist_stored "
             "bias_loaded v_cleared prep mv veps gated rstd sc mx ex tr ptv pta ot ots on o of ofs wo x_done xn_r xt xth xtl qk q1 rs q2 q3 kept0 kept1 kept2 "
             "packed v vs xb msk norm")
    s = ctx.enter_context(semaphores(nc, "a_", names))
    ev_act = lambda h: h % 4 == 3
    N_EV_ACT = 4
    DRAIN = 14
    B_STEP, W_STEP = 10, 12
    X_STEP = 1
    LOOPS = (NB - 2) // 2

    def stepper(eng, iteration):
        iteration(0, 0, True, True)
        with eng.Fori(0, LOOPS) as i:
            for u in range(2):
                iteration(2 * i + 1 + u, (1 + u) % 2, True, True)
        iteration(NB - 1, (NB - 1) % 2, True, False)
        iteration(NB, NB % 2, False, False)

    def lagged(b, step, lag):
        return (b, step - lag) if step >= lag else (b - 1, step - lag + H)

    def tile(b, half):
        return bass.ds(2 * b + half, 1)

    def real(b):
        return not (isinstance(b, int) and b < 0)

    blk = ctx.enter_context(nc.Block())

    @blk.sync
    def _(sp):
        for n, w in enumerate((wq, wk, wv, wo)):
            sp.dma_start(w_in[:, n, :], w).then_inc(s["w_loaded"], 16)
        x_tiles = x_in.rearrange("b (t p) d -> p (b t) d", p=128)
        sp.dma_start(x[:, 0:2, :], x_tiles[:, 0:2, :]).then_inc(s["x0_loaded"], 16)
        sp.dma_start(rel[0:32, :], rel_emb).then_inc(s["rel_loaded"], 16)
        sp.dma_start(hot[0:33, :], buckets).then_inc(s["hot_loaded"], 16)
        sp.dma_start(x[:, 2:NT, :], x_tiles[:, 2:NT, :]).then_inc(s["x_loaded"], 16)
        sp.dma_start(bo_all[:, :], bo.rearrange("(a d) -> a d", a=1).broadcast_to([128, D])).then_inc(s["bo_loaded"], 16)
        sp.wait_ge(s["dist_copied"], 1)
        sp.dma_start(scratch.ap().rearrange("r h u -> h r u"),
                     dist_bias[:, :].rearrange("h (a u) -> h a u", a=1).broadcast_to([H, SKEW, 384])).then_inc(s["dist_stored"], 16)

        def pack(b, par):
            def at(side, p):
                return ((par * 2 + side) * 3 + place_of(side, p)) * DH * H * N

            def store(p):
                sp.wait_ge(s[f"q{p + 1}"], b + 1)
                for side in range(2):
                    out = bass.AP(tensor=parts, offset=at(side, p), ap=[[N, H], [H * N, DH], [1, N]])
                    sp.dma_start(out, part[p][:, N * side:N * side + N]).then_inc(s[f"kept{p}"], 16)

            def load(run):
                m, count = RUNS[run]
                sp.wait_ge(s[f"kept{run}"], 32 * (b + 1))
                for side in range(2):
                    src = bass.AP(tensor=parts, offset=at(side, PARTS[m][side]), ap=[[H * N, DH * count], [N, H], [1, N]])
                    sp.dma_start(qk_pack[side][par][DH * m:DH * (m + count), :, :], src).then_inc(s["packed"], 16)

            store(0)
            store(1)
            load(0)
            store(2)
            load(1)
            load(2)

        pack(0, 0)

        def iteration(b, par, attend, prep):
            if prep:
                pack(b + 1, 1 - par)
        stepper(sp, iteration)

    @blk.gpsimd
    def _(pool):
        for u in range(2):
            nc.gpsimd.memset(v_pad[u][:, :, :, 0:DH], 0.0)
            nc.gpsimd.memset(v_pad[u][:, :, :, DH + 1:32], 0.0)
            last = nc.gpsimd.memset(v_pad[u][:, :, :, DH:DH + 1], 1.0)
        last.then_inc(s["v_cleared"], 1)
        nc.gpsimd.memset(consts[:, 0:1], EPS)
        nc.gpsimd.memset(consts[:, 1:2], -0.5).then_inc(s["v_cleared"], 1)
        pool.wait_ge(s["v_cleared"], 2)
        nc.gpsimd.memset(rel[32:64, :], -BIG).then_inc(s["msk"], 1)

        def deviations(tiles, batches, count):
            two = lambda c: consts[:, c:c + 1].broadcast_to([128, tiles.stop - tiles.start])
            pool.wait_ge(s["mv"], batches)
            nc.gpsimd.tensor_tensor(rstd[:, 0, tiles], mv[:, tiles, 1], two(0), ALU.add).then_inc(s["veps"], 1)
            pool.wait_ge(s["veps"], count)
            nc.gpsimd.tensor_tensor(rstd[:, 1, tiles], rstd[:, 0, tiles], two(1), ALU.pow).then_inc(s["rstd"], 1)

        def prep(b):
            pool.wait_ge(s["q2"], b + 1)
            if not (isinstance(b, int) and b == 0):
                pool.wait_ge(s["kept2"], 32 * b)
            nc.gpsimd.tensor_tensor(part[2][:, :], rest[:, :], part[1][:, :], ALU.subtract).then_inc(s["q3"], 1)
            pool.wait_ge(s["bo_loaded"], 16)
            pool.wait_ge(s["xn_r"], b + 1)
            nc.gpsimd.tensor_tensor(x[:, bass.ds(2 * b, 2), :], x[:, bass.ds(2 * b, 2), :],
                                    bo_all[:, :].rearrange("p (a d) -> p a d", a=1).broadcast_to([128, NH, D]),
                                    ALU.add).then_inc(s["xb"], 1)
        deviations(slice(0, NH), 1, 1)
        prep(0)
        deviations(slice(NH, 2 * NH), 2, 2)
        deviations(slice(2 * NH, NT), NB, 3)

        def iteration(b, par, attend, pr):
            if pr:
                prep(b + 1)
        stepper(pool, iteration)

    @blk.tensor
    def _(pe):
        pe.wait_ge(s["rel_loaded"], 16)
        pe.wait_ge(s["hot_loaded"], 16)
        pe.wait_ge(s["msk"], 1)
        nc.tensor.matmul(M[0:H, 0:384], rel[0:33, :], hot[0:33, :], start=True, stop=True).then_inc(s["dist_done"], 1)

        def transpose_x(b):
            pe.wait_ge(s["xn_r"], b + 1)
            if isinstance(b, int) and b == 0:
                pe.wait_ge(s["dist_copied"], 1)
            need(pe, s["x_done"], b - 2)
            for half in range(NH):
                last = nc.tensor.transpose(M[:, 128 * half:128 * half + 128], xn[:, half, :], ident[:, :])
            last.then_inc(s["xt"], 1)

        def project(b):
            pe.wait_ge(s["w_split"], 2)
            pe.wait_ge(s["xtl"], b + 1)
            need(pe, s["rs"], b)
            for side in range(2):
                out = QK[:, N * side:N * side + N]
                nc.tensor.matmul(out, w_hi[:, side, :], xt_hi[:, :], start=True, stop=False)
                nc.tensor.matmul(out, w_hi[:, side, :], xt_lo[:, :], start=False, stop=False)
                last = nc.tensor.matmul(out, w_lo[:, side, :], xt_hi[:, :], start=False, stop=True)
            last.then_inc(s["qk"], 1)

        def project_v(b):
            for half in range(NH):
                out, cols = M[:, D * half:D * half + D], slice(128 * half, 128 * half + 128)
                nc.tensor.matmul(out, xt_hi[:, cols], w_hi[:, 2, :], start=True, stop=False)
                nc.tensor.matmul(out, xt_lo[:, cols], w_hi[:, 2, :], start=False, stop=False)
                last = nc.tensor.matmul(out, xt_hi[:, cols], w_lo[:, 2, :], start=False, stop=True)
            last.then_inc(s["v"], 1)

        def scores(b, par, h):
            if h == 0:
                pe.wait_ge(s["packed"], 16 * 2 * len(RUNS) * (b + 1))
            need(pe, s["mx"], H * b + h - 1)
            q, k = qk_pack[0][par][:, h, :], qk_pack[1][par][:, h, :]
            nc.tensor.matmul(S[h % 2][:, 0:128], q[:, 0:128], k[:, 0:128], start=True, stop=True)
            nc.tensor.matmul(S[h % 2][:, 128:384], q[:, 128:256], k[:, :], start=True, stop=True).then_inc(s["sc"], 1)

        def transpose_p(b, h):
            pe.wait_ge(s["ex"], H * b + h + 1)
            if h >= 2:
                g, n = h - 2, b
            else:
                g, n = h + H - 2, b - 1
            if real(n):
                if ev_act(g):
                    need(pe, s["pta"], N_EV_ACT * n + g // 4 + 1)
                else:
                    need(pe, s["ptv"], (H - N_EV_ACT) * n + g - g // 4 + 1)
            for c in range(3):
                last = nc.tensor.transpose(PT[h % 2][:, TB[c]:TB[c] + 128], prob[h % 4][:, 128 * c:128 * c + 128],
                                           ident[:, :])
            last.then_inc(s["tr"], 1)
        TB = (0, 128, 256)

        def attend_v(b, par, j):
            pe.wait_ge(s["pta"], N_EV_ACT * b + j + 1)
            pe.wait_ge(s["ptv"], (H - N_EV_ACT) * b + 3 * j + 3)
            if j == 0:
                pe.wait_ge(s["vs"], b + 1)
            need(pe, s["ots"], GROUPS * b + j)
            for kt, cols, src in ((0, slice(0, 256), slice(0, 256)), (1, slice(128, 256), slice(256, 384))):
                for g in range(GH):
                    h = GH * j + g
                    last = nc.tensor.matmul(OT[32 * g:32 * g + 32, cols], v_pad[par][:, kt, h, :],
                                            prob_t[h % 8][:, src], start=(kt == 0), stop=(kt == 1))
            last.then_inc(s["ot"], 1)

        def turn_o(b, j):
            pe.wait_ge(s["ots"], GROUPS * b + j + 1)
            need(pe, s["o"], GROUPS * b + j)
            for half in range(NH):
                last = nc.tensor.transpose(ON[:, 128 * half:128 * half + 128], o_t[:, 128 * half:128 * half + 128],
                                           ident[:, :])
            last.then_inc(s["on"], 1)

        def turn_back(b, free_of):
            pe.wait_ge(s["o"], GROUPS * (b + 1))
            need(pe, s["vs"], free_of)
            for half in range(NH):
                last = nc.tensor.transpose(M[:, 128 * half:128 * half + 128], o[:, half, :], ident[:, :])
            last.then_inc(s["of"], 1)

        def project_out(b):
            pe.wait_ge(s["ofs"], b + 1)
            for half in range(NH):
                last = nc.tensor.matmul(M[:, D * half:D * half + D], of_t[:, 128 * half:128 * half + 128],
                                        w_in[:, 3, :], start=True, stop=True)
            last.then_inc(s["wo"], 1)

        transpose_x(0)
        project(0)
        project_v(0)

        def iteration(b, par, attend, prep):
            for step in range(H if attend else DRAIN):
                if attend:
                    scores(b, par, step)
                n, h = lagged(b, step, LT)
                if real(n) and (attend or step < LT):
                    transpose_p(n, h)
                n, h = lagged(b, step, LP)
                if h % 4 == 3 and real(n) and (attend or step < LP):
                    attend_v(n, par if step >= LP else 1 - par, h // 4)
                n, h = lagged(b, step, LN_)
                if h % 4 == 3 and real(n) and (attend or step < LN_):
                    turn_o(n, h // 4)
                if step == X_STEP and prep:
                    transpose_x(b + 1)
                if step == X_STEP + 2 and prep:
                    project(b + 1)
                if step == X_STEP + 3 and prep:
                    project_v(b + 1)
                if step == B_STEP and real(b - 1):
                    turn_back(b - 1, b + 2 if prep else 0)
                if step == W_STEP and real(b - 1):
                    project_out(b - 1)
        stepper(pe, iteration)

    @blk.scalar
    def _(act):
        def prep_a(b):
            act.wait_ge(s["xt"], b + 1)
            need(act, s["v"], b)
            nc.scalar.copy(xt_hi[:, :], M[:, 0:N]).then_inc(s["xth"], 1)

        def prep_b(b):
            act.wait_ge(s["qk"], b + 1)
            need(act, s["kept0"], 32 * b)
            nc.scalar.copy(part[0][:, :], QK[:, :]).then_inc(s["q1"], 1)

        def prep_c(b, par):
            act.wait_ge(s["v"], b + 1)
            if isinstance(b, int) and b == 0:
                act.wait_ge(s["v_cleared"], 2)
            need(act, s["ot"], GROUPS * (b - 1))
            nc.scalar.copy(v_pad[par][:, :, :, 0:DH],
                           M[:, 0:NH * D].rearrange("p (t h r) -> p t h r", t=NH, r=DH)).then_inc(s["vs"], 1)

        def prep_d(b):
            act.wait_ge(s["rs"], b + 1)
            need(act, s["kept1"], 32 * b)
            nc.scalar.copy(part[1][:, :], rest[:, :]).then_inc(s["q2"], 1)

        def exps(b, h):
            act.wait_ge(s["mx"], H * b + h + 1)
            nc.scalar.activation(prob[h % 4][:, 0:128], prob[h % 4][:, 0:128], ACT.Exp, bias=shift[:, h % 4, 0:1], scale=-1.0)
            nc.scalar.activation(prob[h % 4][:, 128:384], prob[h % 4][:, 128:384], ACT.Exp, bias=shift[:, h % 4, 1:2],
                                 scale=-1.0).then_inc(s["ex"], 1)

        def copy_p(b, h):
            act.wait_ge(s["tr"], H * b + h + 1)
            if h >= 8:
                need(act, s["ot"], GROUPS * b + (h - 8) // 4 + 1)
            else:
                need(act, s["ot"], GROUPS * (b - 1) + (h + 8) // 4 + 1)
            nc.scalar.copy(prob_t[h % 8][:, :], PT[h % 2][:, 0:384]).then_inc(s["pta"], 1)

        def copy_o(b, j):
            act.wait_ge(s["ot"], GROUPS * b + j + 1)
            need(act, s["on"], GROUPS * b + j)
            nc.scalar.copy(o_t[:, :], OT[:, 0:N]).then_inc(s["ots"], 1)

        prep_a(0)
        prep_b(0)
        prep_c(0, 0)
        prep_d(0)
        act.wait_ge(s["dist_stored"], 16)
        for i in range(0, 128, SKEW):
            skewed = bass.AP(tensor=scratch, offset=127 - i, ap=[[H * 384 - 1, SKEW], [384, H], [1, 256]])
            act.dma_start(bias[i:i + SKEW, :, :], skewed).then_inc(s["bias_loaded"], 16)

        def iteration(b, par, attend, prep):
            for step in range(H if attend else DRAIN):
                if step == X_STEP + 4 and prep:
                    prep_d(b + 1)
                n, h = lagged(b, step, LT)
                if ev_act(h) and real(n) and (attend or step < LT):
                    copy_p(n, h)
                if attend:
                    exps(b, step)
                n, h = lagged(b, step, LP)
                if h % 4 == 3 and real(n) and (attend or step < LP):
                    copy_o(n, h // 4)
                if prep:
                    if step == X_STEP:
                        prep_a(b + 1)
                    if step == X_STEP + 2:
                        prep_b(b + 1)
                    if step == X_STEP + 4:
                        prep_c(b + 1, 1 - par)
                if step == B_STEP and real(b - 1):
                    act.wait_ge(s["of"], b)
                    nc.scalar.copy(of_t[:, :], M[:, 0:N]).then_inc(s["ofs"], 1)
        stepper(act, iteration)

    @blk.vector
    def _(dve):
        dve.wait_ge(s["w_loaded"], 64)
        nc.vector.tensor_copy(w_hi[:, :, :], w_in[:, 0:3, :]).then_inc(s["w_split"], 1)
        dve.wait_ge(s["w_split"], 1)
        nc.vector.tensor_tensor(w_lo[:, :, :], w_in[:, 0:3, :], w_hi[:, :, :].bitcast(F32), ALU.subtract).then_inc(s["w_split"], 1)
        dve.wait_ge(s["dist_done"], 1)
        nc.vector.tensor_scalar(dist_bias[:, :], M[0:H, 0:384], 1.0 / SCALE, None, ALU.mult).then_inc(s["dist_copied"], 1)
        dve.wait_ge(s["x0_loaded"], 16)

        def means(b):
            for half in range(NH):
                last = nc.vector.bn_stats(stat[:, tile(b, half), :].rearrange("p a c -> p (a c)"),
                                          x[:, tile(b, half), :].rearrange("p a c -> p (a c)"))
            last.then_inc(s["prep"], 1)

        def variances(b):
            for half in range(NH):
                last = nc.vector.bn_aggr(mv[:, tile(b, half), :].rearrange("p a c -> p (a c)"),
                                         stat[:, tile(b, half), :].rearrange("p a c -> p (a c)"))
            last.then_inc(s["mv"], 1)

        def prep_n(b):
            dve.wait_ge(s["rstd"], b + 1 if isinstance(b, int) and b < 2 else 3)
            need(dve, s["xt"], b)
            for half in range(NH):
                last = nc.vector.tensor_scalar(xn[:, half, :], x[:, tile(b, half), :].rearrange("p a c -> p (a c)"),
                                               mv[:, tile(b, half), 0:1].rearrange("p a c -> p (a c)"),
                                               rstd[:, 1, tile(b, half)], ALU.subtract, ALU.mult)
            last.then_inc(s["xn_r"], 1)

        def prep_b(b):
            dve.wait_ge(s["xth"], b + 1)
            nc.vector.tensor_tensor(xt_lo[:, :], M[:, 0:N], xt_hi[:, :].bitcast(F32), ALU.subtract).then_inc(s["xtl"], 1)

        def prep_c(b):
            dve.wait_ge(s["q1"], b + 1)
            need(dve, s["q3"], b)
            nc.vector.tensor_tensor(rest[:, :], QK[:, :], part[0][:, :], ALU.subtract).then_inc(s["rs"], 1)

        def add_bias(b, h):
            dve.wait_ge(s["sc"], H * b + h + 1)
            need(dve, s["tr"], H * b + h - 3)
            nc.vector.memset(gate2[:, h % 4:h % 4 + 1], 0.0)
            nc.vector.tensor_tensor_reduce(out=prob[h % 4][:, 0:128], in0=S[h % 2][:, 0:128], in1=bias[:, h, 128:256],
                                           scale=-SCALE, scalar=BIG, op0=ALU.add, op1=ALU.min,
                                           accum_out=shift[:, h % 4, 0:1])
            nc.vector.tensor_tensor_reduce(out=prob[h % 4][:, 128:384], in0=S[h % 2][:, 128:384], in1=bias[:, h, :],
                                           scale=-SCALE, scalar=BIG, op0=ALU.add, op1=ALU.min,
                                           accum_out=shift[:, h % 4, 1:2]).then_inc(s["mx"], 1)

        def copy_p(b, h):
            dve.wait_ge(s["tr"], H * b + h + 1)
            if h >= 8:
                need(dve, s["ot"], GROUPS * b + (h - 8) // 4 + 1)
            else:
                need(dve, s["ot"], GROUPS * (b - 1) + (h + 8) // 4 + 1)
            nc.vector.tensor_copy(prob_t[h % 8][:, :], PT[h % 2][:, 0:384]).then_inc(s["ptv"], 1)

        def normalise(b, j):
            dve.wait_ge(s["on"], GROUPS * b + j + 1)
            turned = ON[:, 0:NH * 128].rearrange("p (t g r) -> p t g r", t=NH, g=GH)
            nc.vector.reciprocal(r_sum[:, :, :], turned[:, :, :, DH]).then_inc(s["norm"], 1)
            dve.wait_ge(s["norm"], GROUPS * b + j + 1)
            if j == 0:
                need(dve, s["of"], b)
            nc.vector.tensor_tensor(
                o[:, :, GH * DH * j:GH * DH * (j + 1)].rearrange("p t (g r) -> p t g r", g=GH), turned[:, :, :, 0:DH],
                r_sum[:, :, :].rearrange("p t (g a) -> p t g a", a=1).broadcast_to([128, NH, GH, DH]),
                ALU.mult).then_inc(s["o"], 1)

        means(0)
        dve.wait_ge(s["prep"], 1)
        nc.vector.memset(gate[:, :], 0.0).then_inc(s["gated"], 1)
        variances(0)
        prep_n(0)
        prep_b(0)
        prep_c(0)
        dve.wait_ge(s["x_loaded"], 16)
        dve.wait_ge(s["gated"], 1)
        nc.vector.memset(gate[:, :], 0.0)
        with dve.Fori(0, (NB - 1) // 3) as i:
            for u in range(3):
                means(3 * i + 1 + u)
        dve.wait_ge(s["prep"], NB)
        nc.vector.memset(gate2[:, 4:5], 0.0)
        for b in range(1, NB):
            variances(b)
        dve.wait_ge(s["bias_loaded"], 16 * 128 // SKEW)

        def iteration(b, par, attend, prep):
            for step in range(H if attend else DRAIN):
                if attend:
                    add_bias(b, step)
                if step == X_STEP + 3 and prep:
                    prep_c(b + 1)
                n, h = lagged(b, step, LT)
                if not ev_act(h) and real(n) and (attend or step < LT):
                    copy_p(n, h)
                n, h = lagged(b, step, LN_)
                if h % 4 == 3 and real(n) and (attend or step < LN_):
                    normalise(n, h // 4)
                if prep:
                    if step == 0:
                        prep_n(b + 1)
                    if step == X_STEP + 1:
                        prep_b(b + 1)
                if step == W_STEP and real(b - 1):
                    dve.wait_ge(s["wo"], b)
                    dve.wait_ge(s["xb"], b)
                    tiles = bass.ds(2 * (b - 1), 2)
                    nc.vector.tensor_tensor(x[:, tiles, :], x[:, tiles, :], M[:, 0:N].rearrange("p (t d) -> p t d", t=NH),
                                            ALU.add).then_inc(s["x_done"], 1)
        stepper(dve, iteration)


def pipelined(eng, iteration, count, depth, lead):
    for it in range(lead):
        iteration(it, it % 2)
    with eng.Fori(0, (count - lead) // 2) as i:
        for u in range(2):
            iteration(2 * i + (lead + u), u)
    for it in range(count, count + depth):
        iteration(it, it % 2)


def within(b, count):
    return not isinstance(b, int) or 0 <= b < count


def expert_choice_ffn(nc, tag, x, ident, gate_w, wg, wu, wd, ws_g, ws_u, ws_d, slots):
    E, F, CAP = 16, 256, 32
    FT = F // 128
    EC = E * CAP
    JE = 128 // CAP
    NJ = E // JE
    BG = 128 // E
    NG = NB // BG

    with ExitStack() as ctx:
        def sb(name, shape, dt=F32):
            return ctx.enter_context(nc.sbuf_tensor(tag + name, shape, dt))

        logits = sb("logits", [128, NH, NB, E])
        weight = sb("weight", [128, NH, NB, E])
        place = sb("place", [128, NH, NB, E])
        slot = sb("slot", [128, CAP])
        xn_all = sb("xn_all", [128, NT, D])

        with ExitStack() as sub:
            normalise_and_share(nc, tag + "s_", sub, x, ident, gate_w, ws_g, ws_u, ws_d, slots, logits, xn_all, slot,
                                E, F, FT, CAP)
        with ExitStack() as sub:
            route(nc, tag + "r_", sub, ident, logits, weight, place, E, CAP, BG, NG)
        with ExitStack() as mid:
            eo_all = mid.enter_context(nc.sbuf_tensor(tag + "eo_all", [128, NB, NJ, D], F32))
            eo = [mid.enter_context(nc.sbuf_tensor(tag + f"eo{u}", [128, NB * CAP // 128, D], F32)) for u in range(2)]
            moved = mid.enter_context(semaphores(nc, tag, "moved0 moved1"))
            with ExitStack() as sub:
                xg_hi = sub.enter_context(nc.sbuf_tensor(tag + "xg_hi", [128, E, NB, CAP], F32R))
                xg_lo = sub.enter_context(nc.sbuf_tensor(tag + "xg_lo", [128, E, NB, CAP], F32R))
                weights = ExpertWeights(nc, tag + "w_", sub, wg, wu, wd, F, FT)
                with ExitStack() as inner:
                    gather(nc, tag + "g_", inner, xn_all, place, slot, xg_hi, xg_lo, weights, E, CAP)
                with ExitStack() as inner:
                    experts(nc, tag + "e_", inner, xg_hi, xg_lo, weights, eo, eo_all, moved, E, F, FT, CAP)
            with ExitStack() as sub:
                combine(nc, tag + "c_", sub, x, ident, place, weight, slot, eo, eo_all, moved, E, CAP, NJ)


def normalise_and_share(nc, tag, ctx, x, ident, gate_w, ws_g, ws_u, ws_d, slots, logits, xn_all, slot, E, F, FT, CAP):
    sb = lambda name, shape, dt=F32: ctx.enter_context(nc.sbuf_tensor(tag + name, shape, dt))
    bank = lambda name: ctx.enter_context(nc.psum_tensor(tag + name, [128, 512], F32))
    C = 2 * F + E
    w_in, w_hi, w_lo = sb("w_in", [128, C]), sb("w_hi", [128, C], F32R), sb("w_lo", [128, C], F32R)
    w_down = sb("w_down", [128, FT, D])
    consts, gate = sb("consts", [128, 2]), sb("gate", [128, 1])
    stat, mv, rstd = sb("stat", [128, NH, 6]), sb("mv", [128, 2, NH, 2]), sb("rstd", [128, 2, 2, NH])
    xn = [sb(f"xn{u}", [128, NH, D]) for u in range(2)]
    xt_hi = [sb(f"xt_hi{u}", [128, N], F32R) for u in range(2)]
    xt_lo = [sb(f"xt_lo{u}", [128, N], F32R) for u in range(2)]
    act_g = [sb(f"act_g{u}", [128, FT, N]) for u in range(2)]
    hid = [sb(f"hid{u}", [128, FT, N]) for u in range(2)]
    XT, G, U = ([bank(n + str(u)) for u in range(2)] for n in ("XT", "G", "U"))
    L, Y = bank("L"), bank("Y")
    names = "w_loaded d_loaded split ready mv veps rstd prep xn kept xt xth xtl gu lg lgc gel hid y xadd"
    s = ctx.enter_context(semaphores(nc, tag, names))
    blk = ctx.enter_context(nc.Block())
    DEPTH, LEAD = 5, 6

    @blk.sync
    def _(sp):
        for src, at in ((ws_g, 0), (ws_u, F), (gate_w, 2 * F)):
            sp.dma_start(w_in[:, at:at + src.shape[1]], src).then_inc(s["w_loaded"], 16)
        sp.dma_start(slot[:, :], slots.rearrange("(a c) -> a c", a=1).broadcast_to([128, CAP])).then_inc(s["d_loaded"], 16)
        sp.dma_start(w_down[:, :, :], ws_d.rearrange("(t p) d -> p t d", p=128)).then_inc(s["d_loaded"], 16)

    @blk.gpsimd
    def _(pool):
        nc.gpsimd.memset(consts[:, 0:1], EPS)
        nc.gpsimd.memset(consts[:, 1:2], -0.5).then_inc(s["ready"], 1)
        pool.wait_ge(s["ready"], 1)

        def iteration(it, par):
            if within(it, NB):
                pool.wait_ge(s["mv"], it + 1)
                need(pool, s["xn"], it - 1)
                rstd_tiles(nc, pool, mv[:, par], consts, rstd[:, par], s["veps"], it + 1).then_inc(s["rstd"], 1)
            b = it - 1
            if within(b, NB):
                pool.wait_ge(s["xn"], b + 1)
                nc.gpsimd.tensor_copy(xn_all[:, bass.ds(2 * b, NH), :], xn[1 - par][:, :, :]).then_inc(s["kept"], 1)
        pipelined(pool, iteration, NB, DEPTH, LEAD)
        pool.wait_ge(s["kept"], NB)

    @blk.vector
    def _(dve):
        def iteration(it, par):
            b = it - 5
            if within(b, NB):
                dve.wait_ge(s["y"], b + 1)
                nc.vector.tensor_tensor(x[:, bass.ds(2 * b, NH), :], x[:, bass.ds(2 * b, NH), :],
                                        Y[:, 0:N].rearrange("p (t d) -> p t d", t=NH), ALU.add).then_inc(s["xadd"], 1)
            b = it - 4
            if within(b, NB):
                dve.wait_ge(s["gel"], b + 1)
                need(dve, s["y"], b - 1)
                nc.vector.tensor_tensor(hid[par][:, :, :], act_g[par][:, :, :],
                                        U[par][:, :].rearrange("p (t s) -> p t s", t=FT), ALU.mult).then_inc(s["hid"], 1)
            b = it - 1
            if within(b, NB):
                dve.wait_ge(s["rstd"], b + 1)
                need(dve, s["xt"], b - 1)
                need(dve, s["kept"], b - 1)
                norm_tiles(nc, x, b, mv[:, 1 - par], rstd[:, 1 - par], xn[1 - par]).then_inc(s["xn"], 1)
            if within(it, NB):
                chain = Chain(dve, s["prep"], 3, it)
                stats_tiles(nc, dve, chain, x, it, stat, mv[:, par], gate).then_inc(s["mv"], 1)
                chain.close()
            b = it - 2
            if isinstance(b, int) and b == 0:
                dve.wait_ge(s["split"], 1)
                nc.vector.tensor_tensor(w_lo[:, :], w_in[:, :], w_hi[:, :].bitcast(F32), ALU.subtract).then_inc(s["split"], 1)
            if within(b, NB):
                dve.wait_ge(s["xth"], b + 1)
                need(dve, s["lg"], b - 1)
                nc.vector.tensor_tensor(xt_lo[par][:, :], XT[par][:, 0:N], xt_hi[par][:, :].bitcast(F32),
                                        ALU.subtract).then_inc(s["xtl"], 1)
        pipelined(dve, iteration, NB, DEPTH, LEAD)

    @blk.scalar
    def _(act):
        act.wait_ge(s["w_loaded"], 48)
        nc.scalar.copy(w_hi[:, :], w_in[:, :]).then_inc(s["split"], 1)

        def iteration(it, par):
            b = it - 3
            if within(b, NB):
                act.wait_ge(s["gu"], b + 1)
                need(act, s["hid"], b - 1)
                nc.scalar.activation(act_g[1 - par][:, :, :], G[1 - par][:, :].rearrange("p (t s) -> p t s", t=FT),
                                     ACT.Gelu).then_inc(s["gel"], 1)
                act.wait_ge(s["lg"], b + 1)
                nc.scalar.copy(logits[:, :, bass.ds(b, 1), :].rearrange("p t a e -> p t (a e)"),
                               L[:, 0:NH * E].rearrange("p (t e) -> p t e", t=NH)).then_inc(s["lgc"], 1)
            b = it - 1
            if within(b, NB):
                act.wait_ge(s["xt"], b + 1)
                need(act, s["lg"], b - 1)
                nc.scalar.copy(xt_hi[1 - par][:, :], XT[1 - par][:, 0:N]).then_inc(s["xth"], 1)
        pipelined(act, iteration, NB, DEPTH, LEAD)

    @blk.tensor
    def _(pe):

        def iteration(it, par):
            b = it - 3
            if isinstance(b, int) and b == 0:
                pe.wait_ge(s["d_loaded"], 32)
                pe.wait_ge(s["split"], 2)
            if within(b, NB):
                pe.wait_ge(s["xtl"], b + 1)
                need(pe, s["hid"], b - 1)
                for bank_, at in ((G[1 - par], 0), (U[1 - par], F)):
                    for t in range(FT):
                        out, cols = bank_[:, N * t:N * t + N], slice(at + 128 * t, at + 128 * t + 128)
                        nc.tensor.matmul(out, w_hi[:, cols], xt_hi[1 - par][:, :], start=True, stop=False)
                        nc.tensor.matmul(out, w_hi[:, cols], xt_lo[1 - par][:, :], start=False, stop=False)
                        last = nc.tensor.matmul(out, w_lo[:, cols], xt_hi[1 - par][:, :], start=False, stop=True)
                last.then_inc(s["gu"], 1)
                need(pe, s["lgc"], b)
                for half in range(NH):
                    out, rows, cols = L[:, E * half:E * half + E], slice(128 * half, 128 * half + 128), slice(2 * F, C)
                    nc.tensor.matmul(out, xt_hi[1 - par][:, rows], w_hi[:, cols], start=True, stop=False)
                    nc.tensor.matmul(out, xt_lo[1 - par][:, rows], w_hi[:, cols], start=False, stop=False)
                    last = nc.tensor.matmul(out, xt_hi[1 - par][:, rows], w_lo[:, cols], start=False, stop=True)
                last.then_inc(s["lg"], 1)
            b = it - 4
            if within(b, NB):
                pe.wait_ge(s["hid"], b + 1)
                need(pe, s["xadd"], b)
                for half in range(NH):
                    for t in range(FT):
                        last = nc.tensor.matmul(Y[:, D * half:D * half + D], hid[par][:, t, 128 * half:128 * half + 128],
                                                w_down[:, t, :], start=(t == 0), stop=(t == FT - 1))
                last.then_inc(s["y"], 1)
            b = it - 1
            if within(b, NB):
                pe.wait_ge(s["xn"], b + 1)
                need(pe, s["xtl"], b - 1)
                for half in range(NH):
                    last = nc.tensor.transpose(XT[1 - par][:, 128 * half:128 * half + 128], xn[1 - par][:, half, :],
                                               ident[:, :])
                last.then_inc(s["xt"], 1)
        pipelined(pe, iteration, NB, DEPTH, LEAD)


def route(nc, tag, ctx, ident, logits, weight, place, E, CAP, BG, NG):
    sb = lambda name, shape, dt=F32: ctx.enter_context(nc.sbuf_tensor(tag + name, shape, dt))
    top, low, total = sb("top", [128, NT]), sb("low", [128, NT, E]), sb("total", [128, 2, NT])
    left = [sb(f"left{n}", [128, NG, N]) for n in range(2)]
    best = [sb(f"best{n}", [128, 8]) for n in range(NG)]
    chosen, count, ones = sb("chosen", [128, NG, N]), sb("count", [128, NG, N]), sb("ones", [128, N])
    ranked = sb("ranked", [128, NG, N])
    W = [ctx.enter_context(nc.psum_tensor(tag + f"W{g}", [128, 512], F32)) for g in range(NG)]
    P = [ctx.enter_context(nc.psum_tensor(tag + f"P{g}", [128, 512], F32)) for g in range(NG)]
    s = ctx.enter_context(semaphores(nc, tag, "low exped link weighed turned back"))
    blk = ctx.enter_context(nc.Block())
    flat = lambda t: t[:, :, :, :].rearrange("p t b e -> p (t b) e")
    over = lambda ap: ap.rearrange("p (t a) -> p t a", a=1).broadcast_to([128, NT, E])

    @blk.scalar
    def _(act):
        act.wait_ge(s["low"], 1)
        nc.scalar.activation(low[:, :, :], low[:, :, :], ACT.Exp).then_inc(s["exped"], 1)

    @blk.tensor
    def _(pe):
        pe.wait_ge(s["weighed"], 1)
        for g in range(NG):
            for half in range(NH):
                tiles = weight[:, half, BG * g:BG * (g + 1), :].rearrange("p b e -> p (b e)")
                last = nc.tensor.transpose(W[g][:, 128 * half:128 * half + 128], tiles, ident[:, :])
            last.then_inc(s["turned"], 1)
        for g in range(NG):
            pe.wait_ge(s["back"], g + 1)
            for half in range(NH):
                last = nc.tensor.transpose(P[g][:, 128 * half:128 * half + 128], ranked[:, g, 128 * half:128 * half + 128],
                                           ident[:, :])
            last.then_inc(s["turned"], 1)

    @blk.vector
    def _(dve):
        done = [0]

        def link(ins):
            done[0] += 1
            ins.then_inc(s["link"], 1)
            dve.wait_ge(s["link"], done[0])

        link(nc.vector.tensor_reduce(top[:, :], flat(logits), AX.X, ALU.max))
        nc.vector.tensor_tensor(low[:, :, :], flat(logits), over(top[:, :]), ALU.subtract).then_inc(s["low"], 1)
        nc.vector.memset(ones[:, :], 1.0)
        dve.wait_ge(s["exped"], 1)
        link(nc.vector.tensor_reduce(total[:, 0, :], low[:, :, :], AX.X, ALU.add))
        link(nc.vector.reciprocal(total[:, 1, :], total[:, 0, :]))
        nc.vector.tensor_tensor(flat(weight), low[:, :, :], over(total[:, 1, :]), ALU.mult).then_inc(s["weighed"], 1)
        for g in range(NG):
            dve.wait_ge(s["turned"], g + 1)
            last = nc.vector.tensor_copy(left[0][:, g, :], W[g][:, 0:N])
        link(last)
        for r in range(CAP // 8):
            for g in range(NG):
                last = nc.vector.max(best[g][:, :], left[r % 2][:, g, :])
            link(last)
            for g in range(NG):
                last = nc.vector.match_replace(left[1 - r % 2][:, g, :], best[g][:, :], left[r % 2][:, g, :], -1.0)
            link(last)
        link(nc.vector.tensor_scalar(chosen[:, :, :], left[(CAP // 8) % 2][:, :, :], 0.0, None, ALU.is_lt))
        for g in range(NG):
            last = nc.vector.tensor_tensor_scan(count[:, g, :], ones[:, :], chosen[:, g, :], 0.0, ALU.mult, ALU.add)
        link(last)
        for g in range(NG):
            nc.vector.tensor_tensor(ranked[:, g, :], count[:, g, :], chosen[:, g, :], ALU.mult).then_inc(s["back"], 1)
        for g in range(NG):
            dve.wait_ge(s["turned"], NG + g + 1)
            for half in range(NH):
                tiles = place[:, half, BG * g:BG * (g + 1), :].rearrange("p b e -> p (b e)")
                nc.vector.tensor_copy(tiles, P[g][:, 128 * half:128 * half + 128])


def is_in_slot(nc, out, place, slot, half, b, E, CAP):
    at = place[:, half, bass.ds(b, 1), :].rearrange("p a (e b) -> p (a e) b", b=1).broadcast_to([128, E, CAP])
    all_slots = slot[:, :].rearrange("p (a c) -> p a c", a=1).broadcast_to([128, E, CAP])
    return nc.vector.tensor_tensor(out, at, all_slots, ALU.is_equal)


class ExpertWeights:
    SETS, SPLITS = 4, 2
    EARLY = 2

    def __init__(self, nc, tag, ctx, wg, wu, wd, F, FT):
        sb = lambda name, shape, dt=F32: ctx.enter_context(nc.sbuf_tensor(tag + name, shape, dt))
        self.nc, self.wg, self.wu, self.wd = nc, wg, wu, wd
        self.w_in = [sb(f"w_in{u}", [128, 2, F]) for u in range(self.SETS)]
        self.w_hi = [sb(f"w_hi{u}", [128, 2, F], F32R) for u in range(self.SPLITS)]
        self.w_lo = [sb(f"w_lo{u}", [128, 2, F], F32R) for u in range(self.SPLITS)]
        self.w_down = [sb(f"w_down{u}", [128, FT, D]) for u in range(self.SETS)]
        self.s = ctx.enter_context(semaphores(nc, tag, "w_in0 w_in1 w_in2 w_in3 wd0 wd1 wd2 wd3 w_hi w_lo"))

    def load_gates(self, sp, e, u):
        for k, w in enumerate((self.wg, self.wu)):
            sp.dma_start(self.w_in[u][:, k, :], w[bass.ds(e, 1), :, :].rearrange("a p f -> p (a f)")).then_inc(self.s[f"w_in{u}"], 16)

    def load_down(self, sp, e, u):
        sp.dma_start(self.w_down[u][:, :, :], self.wd[bass.ds(e, 1), :, :].rearrange("a (t p) d -> p (a t) d", p=128)).then_inc(self.s[f"wd{u}"], 16)

    def split_high(self, act, u, turn):
        act.wait_ge(self.s[f"w_in{u}"], 32 * (turn + 1))
        self.nc.scalar.copy(self.w_hi[u % 2][:, :, :], self.w_in[u][:, :, :]).then_inc(self.s["w_hi"], 1)

    def split_low(self, pool, e, u):
        pool.wait_ge(self.s["w_hi"], e + 1)
        self.nc.gpsimd.tensor_tensor(self.w_lo[u % 2][:, :, :], self.w_in[u][:, :, :],
                                     self.w_hi[u % 2][:, :, :].bitcast(F32), ALU.subtract).then_inc(self.s["w_lo"], 1)


def gather(nc, tag, ctx, xn_all, place, slot, xg_hi, xg_lo, weights, E, CAP):
    sb = lambda name, shape, dt=F32: ctx.enter_context(nc.sbuf_tensor(tag + name, shape, dt))
    bank = lambda name: ctx.enter_context(nc.psum_tensor(tag + name, [128, 512], F32))
    xs_hi = [sb(f"xs_hi{u}", [128, NH, D], F32R) for u in range(2)]
    xs_lo = [sb(f"xs_lo{u}", [128, NH, D], F32R) for u in range(2)]
    hot = [[sb(f"hot{u}{half}", [128, E, CAP], F32R) for half in range(NH)] for u in range(2)]
    XH, XL = ([bank(n + str(u)) for u in range(2)] for n in ("XH", "XL"))
    s = ctx.enter_context(semaphores(nc, tag, "hi lo hot got outh outl"))
    blk = ctx.enter_context(nc.Block())
    DEPTH, LEAD = 2, 4

    @blk.sync
    def _(sp):
        for e in range(weights.EARLY):
            weights.load_gates(sp, e, e)
            weights.load_down(sp, e, e)

    @blk.gpsimd
    def _(pool):
        def iteration(it, par):
            if within(it, NB):
                pool.wait_ge(s["hi"], it + 1)
                need(pool, s["got"], it - 1)
                nc.gpsimd.tensor_tensor(xs_lo[par][:, :, :], xn_all[:, bass.ds(2 * it, NH), :],
                                        xs_hi[par][:, :, :].bitcast(F32), ALU.subtract).then_inc(s["lo"], 1)
            if isinstance(it, int) and NB <= it < NB + weights.EARLY:
                weights.split_low(pool, it - NB, it - NB)
        pipelined(pool, iteration, NB, DEPTH, LEAD)

    @blk.scalar
    def _(act):
        def iteration(it, par):
            if within(it, NB):
                need(act, s["got"], it - 1)
                nc.scalar.copy(xs_hi[par][:, :, :], xn_all[:, bass.ds(2 * it, NH), :]).then_inc(s["hi"], 1)
            if isinstance(it, int) and 2 <= it < 2 + weights.EARLY:
                weights.split_high(act, it - 2, 0)
            b = it - 2
            if within(b, NB):
                act.wait_ge(s["got"], b + 1)
                nc.scalar.copy(xg_hi[:, :, bass.ds(b, 1), :].rearrange("p e a c -> p e (a c)"),
                               XH[par][:, :].rearrange("p (e c) -> p e c", c=CAP)).then_inc(s["outh"], 1)
                nc.scalar.copy(xg_lo[:, :, bass.ds(b, 1), :].rearrange("p e a c -> p e (a c)"),
                               XL[par][:, :].rearrange("p (e c) -> p e c", c=CAP)).then_inc(s["outl"], 1)
        pipelined(act, iteration, NB, DEPTH, LEAD)

    @blk.vector
    def _(dve):
        def iteration(it, par):
            if within(it, NB):
                need(dve, s["got"], it - 1)
                for half in range(NH):
                    last = is_in_slot(nc, hot[par][half][:, :, :], place, slot, half, it, E, CAP)
                last.then_inc(s["hot"], 1)
        pipelined(dve, iteration, NB, DEPTH, LEAD)

    @blk.tensor
    def _(pe):
        def iteration(it, par):
            if within(it, NB):
                for n in ("hot", "lo"):
                    pe.wait_ge(s[n], it + 1)
                need(pe, s["outh"], it - 1)
                need(pe, s["outl"], it - 1)
                for out, xs in ((XH[par], xs_hi[par]), (XL[par], xs_lo[par])):
                    for half in range(NH):
                        last = nc.tensor.matmul(out[:, :], xs[:, half, :], hot[par][half][:, :, :],
                                                start=(half == 0), stop=(half == NH - 1))
                last.then_inc(s["got"], 1)
        pipelined(pe, iteration, NB, DEPTH, LEAD)


def move_rows(sp, eo, eo_all, moved, CAP, u, i):
    for r in range(128 // CAP):
        sp.dma_start(eo_all[CAP * u:CAP * u + CAP, r::4, bass.ds(i, 1), :].rearrange("p b a d -> p b (a d)"),
                     eo[u % 2][CAP * r:CAP * r + CAP, :, :]).then_inc(moved[f"moved{u % 2}"], 16)


def experts(nc, tag, ctx, xg_hi, xg_lo, weights, eo, eo_all, moved, E, F, FT, CAP):
    S = NB * CAP
    ST = S // 128
    UNROLL = 4
    sb = lambda name, shape, dt=F32: ctx.enter_context(nc.sbuf_tensor(tag + name, shape, dt))
    bank = lambda name: ctx.enter_context(nc.psum_tensor(tag + name, [128, 512], F32))
    w_hi, w_lo, w_down = weights.w_hi, weights.w_lo, weights.w_down
    act_g = sb("act_g", [128, FT, S])
    hid = [sb(f"hid{u}", [128, FT, S]) for u in range(2)]
    G, U, Y = ([bank(n + str(t)) for t in range(2)] for n in ("G", "U", "Y"))
    s = ctx.enter_context(semaphores(nc, tag, "gu gel hid y eo"))
    blk = ctx.enter_context(nc.Block())

    def turns(eng, iteration):
        for e in range(UNROLL):
            iteration(e, e, 0)
        with eng.Fori(1, E // UNROLL) as i:
            for u in range(UNROLL):
                iteration(UNROLL * i + u, u, i)
        iteration(E, 0, E // UNROLL)

    def half_count(e, u, i):
        return (UNROLL // 2) * i + u // 2 + 1

    @blk.sync
    def _(sp):
        def load(e, u, i):
            a, c = values(sp, e, e - 3)
            need(sp, weights.s["w_lo"], c)
            weights.load_gates(sp, a, u)
            need(sp, s["y"], c)
            weights.load_down(sp, a, u)

        def iteration(e, u, i):
            if not (isinstance(e, int) and e + 2 >= E):
                load(e + 2, (u + 2) % UNROLL, i + (u + 2) // UNROLL)
            if not (isinstance(e, int) and e == 0):
                v, = values(sp, e)
                sp.wait_ge(s["eo"], v)
                move_rows(sp, eo, eo_all, moved, CAP, (u - 1) % UNROLL, i - 1 if u == 0 else i)

        for e in range(UNROLL):
            iteration(e, e, 0)
        with sp.Fori(1, E // UNROLL - 1) as i:
            for u in range(UNROLL):
                iteration(UNROLL * i + u, u, i)
        for e in range(E - UNROLL, E):
            iteration(e, e % UNROLL, E // UNROLL - 1)

    @blk.scalar
    def _(act):
        def iteration(e, u, i):
            if within(e, E) and not (isinstance(e, int) and e < weights.EARLY):
                act.wait_ge(s["gu"], FT * (e - 1))
                weights.split_high(act, u, i)
            e, u = e - 1, (u - 1) % UNROLL
            if within(e, E):
                for t in range(FT):
                    act.wait_ge(s["gu"], FT * e + t + 1)
                    need(act, s["hid"], FT * (e - 1) + t + 1)
                    nc.scalar.activation(act_g[:, t, :], G[t][:, :], ACT.Gelu).then_inc(s["gel"], 1)
        turns(act, iteration)

    @blk.gpsimd
    def _(pool):
        def iteration(e, u, i):
            if within(e, E) and not (isinstance(e, int) and e < weights.EARLY):
                weights.split_low(pool, e, u)
        turns(pool, iteration)

    @blk.vector
    def _(dve):
        def down(e, u, i):
            dve.wait_ge(s["y"], e + 1)
            n = half_count(e, u, i)
            need(dve, moved[f"moved{u % 2}"], 64 * (n - 1))
            nc.vector.tensor_copy(eo[u % 2][:, :, :], Y[u % 2][:, :].rearrange("p (t d) -> p t d", t=ST)).then_inc(s["eo"], 1)

        def iteration(e, u, i):
            if not (isinstance(e, int) and e == 0):
                e1, u1 = e - 1, (u - 1) % UNROLL
                for t in range(FT):
                    dve.wait_ge(s["gel"], FT * e1 + t + 1)
                    need(dve, s["y"], e1 - 1)
                    nc.vector.tensor_tensor(hid[u1 % 2][:, t, :], act_g[:, t, :], U[t][:, :], ALU.mult).then_inc(s["hid"], 1)
            if not (isinstance(e, int) and e < 2):
                u2 = (u - 2) % UNROLL
                down(e - 2, u2, i - 1 if u < 2 else i)
        turns(dve, iteration)
        down(E - 1, UNROLL - 1, E // UNROLL - 1)

    @blk.tensor
    def _(pe):
        def down(e, u, i):
            pe.wait_ge(s["hid"], FT * (e + 1))
            pe.wait_ge(weights.s[f"wd{u}"], 16 * (i + 1))
            need(pe, s["eo"], e - 1)
            for st in range(ST):
                for t in range(FT):
                    last = nc.tensor.matmul(Y[u % 2][:, D * st:D * st + D], hid[u % 2][:, t, 128 * st:128 * st + 128],
                                            w_down[u][:, t, :], start=(t == 0), stop=(t == FT - 1))
            last.then_inc(s["y"], 1)

        def iteration(e, u, i):
            if within(e, E):
                pe.wait_ge(weights.s["w_lo"], e + 1)
                hi = xg_hi[:, bass.ds(e, 1), :, :].rearrange("p a b c -> p (a b c)")
                lo = xg_lo[:, bass.ds(e, 1), :, :].rearrange("p a b c -> p (a b c)")
                for t in range(FT):
                    need(pe, s["hid"], FT * (e - 1) + t + 1)
                    for k, bank_ in enumerate((G[t], U[t])):
                        cols = slice(128 * t, 128 * t + 128)
                        nc.tensor.matmul(bank_[:, :], w_hi[u % 2][:, k, cols], hi, start=True, stop=False)
                        nc.tensor.matmul(bank_[:, :], w_hi[u % 2][:, k, cols], lo, start=False, stop=False)
                        last = nc.tensor.matmul(bank_[:, :], w_lo[u % 2][:, k, cols], hi, start=False, stop=True)
                    last.then_inc(s["gu"], 1)
            if not (isinstance(e, int) and e == 0):
                down(e - 1, (u - 1) % UNROLL, i - 1 if u == 0 else i)
        turns(pe, iteration)


def combine(nc, tag, ctx, x, ident, place, weight, slot, eo, eo_all, moved, E, CAP, NJ):
    sb = lambda name, shape, dt=F32: ctx.enter_context(nc.sbuf_tensor(tag + name, shape, dt))
    bank = lambda name: ctx.enter_context(nc.psum_tensor(tag + name, [128, 512], F32))
    hot = [sb(f"hot{u}", [128, NH, E, CAP]) for u in range(2)]
    mix = [sb(f"mix{u}", [128, NH, E, CAP]) for u in range(2)]
    mix_t = [sb(f"mix_t{u}", [128, NJ, N]) for u in range(2)]
    T = [[bank(f"T{u}{k}") for k in range(2)] for u in range(2)]
    Y = [bank(f"Y{u}") for u in range(2)]
    s = ctx.enter_context(semaphores(nc, tag, "hot mix t0 t1 ta tv y xadd"))
    blk = ctx.enter_context(nc.Block())
    DEPTH, LEAD = 4, 6

    @blk.sync
    def _(sp):
        move_rows(sp, eo, eo_all, moved, CAP, (E - 1) % 4, (E - 1) // 4)

    @blk.gpsimd
    def _(pool):
        def iteration(it, par):
            if within(it, NB):
                pool.wait_ge(s["hot"], it + 1)
                need(pool, s["t1"], it - 1)
                w = weight[:, :, bass.ds(it, 1), :].rearrange("p t a e -> p t e a").broadcast_to([128, NH, E, CAP])
                nc.gpsimd.tensor_tensor(mix[par][:, :, :, :], hot[par][:, :, :, :], w, ALU.mult).then_inc(s["mix"], 1)
        pipelined(pool, iteration, NB, DEPTH, LEAD)

    @blk.vector
    def _(dve):
        def iteration(it, par):
            if within(it, NB):
                need(dve, s["mix"], it - 1)
                for half in range(NH):
                    last = is_in_slot(nc, hot[par][:, half, :, :], place, slot, half, it, E, CAP)
                last.then_inc(s["hot"], 1)
            b = it - 2
            if within(b, NB):
                dve.wait_ge(s["t1"], b + 1)
                need(dve, s["y"], b - 1)
                nc.vector.tensor_copy(mix_t[par][:, 2:4, :], T[par][1][:, :].rearrange("p (j s) -> p j s", j=2)).then_inc(s["tv"], 1)
            b = it - 4
            if within(b, NB):
                dve.wait_ge(s["y"], b + 1)
                nc.vector.tensor_tensor(x[:, bass.ds(2 * b, NH), :], x[:, bass.ds(2 * b, NH), :],
                                        Y[par][:, 0:N].rearrange("p (t d) -> p t d", t=NH), ALU.add).then_inc(s["xadd"], 1)
        pipelined(dve, iteration, NB, DEPTH, LEAD)

    @blk.scalar
    def _(act):
        def iteration(it, par):
            b = it - 2
            if within(b, NB):
                act.wait_ge(s["t0"], b + 1)
                need(act, s["y"], b - 1)
                nc.scalar.copy(mix_t[par][:, 0:2, :], T[par][0][:, :].rearrange("p (j s) -> p j s", j=2)).then_inc(s["ta"], 1)
        pipelined(act, iteration, NB, DEPTH, LEAD)

    @blk.tensor
    def _(pe):
        def iteration(it, par):
            b = it - 1
            if within(b, NB):
                pe.wait_ge(s["mix"], b + 1)
                for k, (freed, signal) in enumerate((("ta", "t0"), ("tv", "t1"))):
                    need(pe, s[freed], b - 1)
                    for j in range(2 * k, 2 * k + 2):
                        for half in range(NH):
                            at = N * (j % 2) + 128 * half
                            last = nc.tensor.transpose(
                                T[1 - par][k][:, at:at + 128],
                                mix[1 - par][:, half, 4 * j:4 * j + 4, :].rearrange("p e c -> p (e c)"), ident[:, :])
                    last.then_inc(s[signal], 1)
            b = it - 3
            if isinstance(b, int) and b == 0:
                for u in range(2):
                    pe.wait_ge(moved[f"moved{u}"], 64 * E // 2)
            if within(b, NB):
                pe.wait_ge(s["ta"], b + 1)
                pe.wait_ge(s["tv"], b + 1)
                need(pe, s["xadd"], b - 1)
                for half in range(NH):
                    for j in range(NJ):
                        rows = eo_all[:, bass.ds(b, 1), j, :].rearrange("p a d -> p (a d)")
                        last = nc.tensor.matmul(Y[1 - par][:, D * half:D * half + D],
                                                mix_t[1 - par][:, j, 128 * half:128 * half + 128], rows,
                                                start=(j == 0), stop=(j == NJ - 1))
                last.then_inc(s["y"], 1)
        pipelined(pe, iteration, NB, DEPTH, LEAD)


def rotary_attention(nc, ctx, x, ident, wqk, wv, wout, bout, cos, sin):
    H, DH = 16, 64
    PAIRS = H // 2
    W = 2 * N
    LI, LS, LT, LP, LO = 1, 2, 4, 6, 7

    def sb(name, shape, dt=F32):
        return ctx.enter_context(nc.sbuf_tensor("b_" + name, shape, dt))

    def bank(name):
        return ctx.enter_context(nc.psum_tensor("b_" + name, [128, 512], F32))

    CW = 3 * H * DH
    VC = 2 * H * DH
    FIRST = 512
    W_PARTS = (slice(0, FIRST), slice(FIRST, VC), slice(VC, CW))
    w_in, w_hi, w_lo = sb("w_in", [128, CW]), sb("w_hi", [128, CW], F32R), sb("w_lo", [128, CW], F32R)
    w_out = sb("w_out", [128, PAIRS, D])
    b_all = sb("b_all", [128, D])
    turn_c, turn_s = sb("turn_c", [128, W]), sb("turn_s", [128, W])
    stat, mv, rstd = sb("stat", [128, NH, 6]), sb("mv", [128, NH, 2]), sb("rstd", [128, 2, NH])
    gate, consts = sb("gate", [128, 1]), sb("consts", [128, 2])
    xn = sb("xn", [128, NH, D])
    xt_hi, xt_lo = sb("xt_hi", [128, N], F32R), sb("xt_lo", [128, N], F32R)
    swapped = [sb(f"swapped{u}", [128, W]) for u in range(2)]
    scaled = [sb(f"scaled{u}", [128, W]) for u in range(2)]
    turned = sb("turned", [128, W])
    qk = [sb(f"qk{u}", [128, W]) for u in range(2)]
    qk_hi, qk_lo = sb("qk_hi", [128, PAIRS, W], F32R), sb("qk_lo", [128, PAIRS, W], F32R)
    v = [sb(f"v{u}", [128, NH, H * DH]) for u in range(2)]
    prob = [sb(f"prob{n}", [128, 2, N]) for n in range(8)]
    prob_t = [sb(f"prob_t{n}", [128, 2, N]) for n in range(4)]
    shift, total, r_sum = sb("shift", [128, 4, 2]), sb("total", [128, 4, 2]), sb("r_sum", [128, 4, 2])
    o_t = sb("o_t", [128, PAIRS, N])
    S, PT = [bank("S0"), bank("S1")], [bank("PT0"), bank("PT1")]
    OT, QK, VY = [bank("OT0"), bank("OT1")], bank("QK"), bank("VY")
    names = ("w0_loaded w1_loaded w2_loaded c_loaded hi split ready prep mv veps rstd xn xb xt xth xtl qkp sw tu qk qh ql vp vs "
             "sc mx ex tr pt rc sc_even sc_odd ot o y xadd")
    s = ctx.enter_context(semaphores(nc, "b_", names))
    LOOPS = (NB - 2) // 2
    DRAIN = 10

    def stepper(eng, iteration):
        iteration(0, 0, True, True)
        with eng.Fori(0, LOOPS) as i:
            for u in range(2):
                iteration(2 * i + 1 + u, (1 + u) % 2, True, True)
        iteration(NB - 1, (NB - 1) % 2, True, False)
        iteration(NB, NB % 2, False, False)

    def lagged(b, step, lag):
        return (b, step - lag) if step >= lag else (b - 1, step - lag + H)

    def due(b, step, lag, attend):
        n, h = lagged(b, step, lag)
        return (n, h) if (not isinstance(n, int) or n >= 0) and (attend or step < lag) else None

    def projected(b, step, lag, prep):
        at = step - lag
        if at % 2 == 0:
            return None
        if at < 5:
            return (b, PAIRS - 2 + at // 2) if within(b, NB) else None
        return (b + 1, at // 2 - 2) if prep else None

    LR, LH = 1, 4
    X_STEP = 3
    V_STEPS = (10, 12, 14, 15)
    Y_STEP = 8
    blk = ctx.enter_context(nc.Block())

    @blk.sync
    def _(sp):
        sp.dma_start(w_in[:, 0:FIRST], wqk[:, 0:FIRST]).then_inc(s["w0_loaded"], 16)
        sp.dma_start(w_in[:, FIRST:VC], wqk[:, FIRST:VC]).then_inc(s["w1_loaded"], 16)
        sp.dma_start(w_in[:, VC:CW], wv).then_inc(s["w2_loaded"], 16)
        sp.dma_start(turn_c[:, :], cos).then_inc(s["c_loaded"], 16)
        sp.dma_start(turn_s[:, :], sin).then_inc(s["c_loaded"], 16)
        sp.dma_start(w_out[:, :, :], wout.rearrange("(t p) d -> p t d", p=128)).then_inc(s["c_loaded"], 16)
        sp.dma_start(b_all[:, :], bout.rearrange("(a d) -> a d", a=1).broadcast_to([128, D])).then_inc(s["c_loaded"], 16)

    @blk.gpsimd
    def _(pool):
        nc.gpsimd.memset(consts[:, 0:1], EPS)
        nc.gpsimd.memset(consts[:, 1:2], -0.5).then_inc(s["ready"], 1)
        pool.wait_ge(s["ready"], 1)

        def prep_r(b):
            pool.wait_ge(s["mv"], b + 1)
            rstd_tiles(nc, pool, mv, consts, rstd, s["veps"], b + 1).then_inc(s["rstd"], 1)

        def prep_x(b):
            pool.wait_ge(s["xn"], b + 1)
            nc.gpsimd.tensor_tensor(x[:, bass.ds(2 * b, 2), :], x[:, bass.ds(2 * b, 2), :],
                                    b_all[:, :].rearrange("p (a d) -> p a d", a=1).broadcast_to([128, NH, D]),
                                    ALU.add).then_inc(s["xb"], 1)

        def rotate(b, p):
            pool.wait_ge(s["sw"], PAIRS * b + p + 1)
            need(pool, s["qk"], PAIRS * b + p)
            nc.gpsimd.tensor_tensor(turned[:, :], swapped[p % 2][:, :], turn_s[:, :], ALU.mult).then_inc(s["tu"], 1)
            pool.wait_ge(s["tu"], PAIRS * b + p + 1)
            need(pool, s["ql"], PAIRS * b + p - 1)
            nc.gpsimd.tensor_tensor(qk[p % 2][:, :], scaled[p % 2][:, :], turned[:, :], ALU.add).then_inc(s["qk"], 1)

        def scale(b, h):
            pool.wait_ge(s["rc"], H * b + h + 1)
            r = r_sum[:, h % 4, :].rearrange("p (t a) -> p t a", a=1).broadcast_to([128, NH, N])
            nc.gpsimd.tensor_tensor(prob[h % 8][:, :, :], prob[h % 8][:, :, :], r, ALU.mult).then_inc(s["sc_even"], 2)

        prep_r(0)
        pool.wait_ge(s["c_loaded"], 64)
        prep_x(0)
        for p in range(PAIRS - 3):
            rotate(0, p)

        def iteration(b, par, attend, prep):
            for step in range(H if attend else DRAIN):
                if (nh := due(b, step, LS, attend)) is not None and nh[1] % 2 == 0:
                    scale(*nh)
                if (pq := projected(b, step, LR, prep)) is not None:
                    rotate(*pq)
                if prep and step == 0:
                    prep_r(b + 1)
                if prep and step == 2:
                    prep_x(b + 1)
        stepper(pool, iteration)

    @blk.tensor
    def _(pe):
        def transpose_x(b):
            pe.wait_ge(s["xn"], b + 1)
            need(pe, s["vs"], 4 * b)
            for half in range(NH):
                last = nc.tensor.transpose(VY[:, 128 * half:128 * half + 128], xn[:, half, :], ident[:, :])
            last.then_inc(s["xt"], 1)

        def project(b, p, bank=QK, banks=1):
            pe.wait_ge(s["xtl"], b + 1)
            need(pe, s["sw"], PAIRS * b + p + 1 - banks)
            for k in range(2):
                out, cols = bank[:, N * k:N * k + N], slice(128 * (2 * p + k), 128 * (2 * p + k) + 128)
                nc.tensor.matmul(out, w_hi[:, cols], xt_hi[:, :], start=True, stop=False)
                nc.tensor.matmul(out, w_hi[:, cols], xt_lo[:, :], start=False, stop=False)
                last = nc.tensor.matmul(out, w_lo[:, cols], xt_hi[:, :], start=False, stop=True)
            last.then_inc(s["qkp"], 1)

        def project_v(b, c):
            pe.wait_ge(s["xtl"], b + 1)
            need(pe, s["vs"], 4 * b + c)
            if c == 0:
                need(pe, s["xadd"], b - 1)
            rows = slice(128 * (c // 2), 128 * (c // 2) + 128)
            cols = slice(VC + 512 * (c % 2), VC + 512 * (c % 2) + 512)
            nc.tensor.matmul(VY[:, :], xt_hi[:, rows], w_hi[:, cols], start=True, stop=False)
            nc.tensor.matmul(VY[:, :], xt_lo[:, rows], w_hi[:, cols], start=False, stop=False)
            nc.tensor.matmul(VY[:, :], xt_hi[:, rows], w_lo[:, cols], start=False, stop=True).then_inc(s["vp"], 1)

        def scores(b, h):
            pe.wait_ge(s["ql"], PAIRS * b + h // 2 + 1)
            need(pe, s["ex"], H * b + h - 1)
            rows = slice(DH * (h % 2), DH * (h % 2) + DH)
            for t in range(NH):
                out, q, k = S[h % 2][:, N * t:N * t + N], slice(128 * t, 128 * t + 128), slice(N, W)
                nc.tensor.matmul(out, qk_hi[rows, h // 2, q], qk_hi[rows, h // 2, k], start=True, stop=False)
                nc.tensor.matmul(out, qk_hi[rows, h // 2, q], qk_lo[rows, h // 2, k], start=False, stop=False)
                last = nc.tensor.matmul(out, qk_lo[rows, h // 2, q], qk_hi[rows, h // 2, k], start=False, stop=True)
            last.then_inc(s["sc"], 1)

        def transpose_p(b, h):
            pe.wait_ge(s[("sc_even", "sc_odd")[h % 2]], H * b + h + 2 - h % 2)
            need(pe, s["pt"], H * b + h - 1)
            for t in range(NH):
                for kt in range(NH):
                    last = nc.tensor.transpose(PT[h % 2][:, N * kt + 128 * t:N * kt + 128 * t + 128],
                                               prob[h % 8][:, t, 128 * kt:128 * kt + 128], ident[:, :])
            last.then_inc(s["tr"], 1)

        def attend_v(b, par, p):
            pe.wait_ge(s["pt"], H * b + 2 * p + 2)
            if p == 0:
                pe.wait_ge(s["vs"], 4 * (b + 1))
            need(pe, s["o"], PAIRS * b + p - 1)
            for kt in range(NH):
                for g in range(2):
                    h = 2 * p + g
                    last = nc.tensor.matmul(OT[p % 2][DH * g:DH * g + DH, 0:N], v[par][:, kt, DH * h:DH * h + DH],
                                            prob_t[h % 4][:, kt, :], start=(kt == 0), stop=(kt == NH - 1))
            last.then_inc(s["ot"], 1)

        def project_out(b):
            pe.wait_ge(s["o"], PAIRS * (b + 1))
            pe.wait_ge(s["vs"], 4 * min(b + 2, NB) if isinstance(b, int) else 4 * (b + 2))
            for half in range(NH):
                for p in range(PAIRS):
                    last = nc.tensor.matmul(VY[:, D * half:D * half + D], o_t[:, p, 128 * half:128 * half + 128],
                                            w_out[:, p, :], start=(p == 0), stop=(p == PAIRS - 1))
            last.then_inc(s["y"], 1)

        transpose_x(0)
        for p in range(PAIRS - 2):
            if p in (0, 2):
                pe.wait_ge(s["split"], 1 + p // 2)
            project(0, p, (QK, OT[1])[p % 2], 2)
            if p == 1:
                pe.wait_ge(s["split"], 3)
            if 1 <= p < 5:
                project_v(0, p - 1)
        pe.wait_ge(s["c_loaded"], 64)

        def iteration(b, par, attend, prep):
            for step in range(H if attend else DRAIN):
                if attend:
                    scores(b, step)
                if (nh := due(b, step, LT, attend)) is not None:
                    transpose_p(*nh)
                if (nh := due(b, step, LP, attend)) is not None and nh[1] % 2:
                    attend_v(nh[0], par if step >= LP else 1 - par, nh[1] // 2)
                if step == Y_STEP and not (isinstance(b, int) and b == 0):
                    project_out(b - 1)
                if step == X_STEP and prep:
                    transpose_x(b + 1)
                if (pq := projected(b, step, 0, prep)) is not None:
                    project(*pq)
                if step in V_STEPS and prep:
                    project_v(b + 1, V_STEPS.index(step))
        stepper(pe, iteration)

    @blk.scalar
    def _(act):
        def split_w(part):
            cols = W_PARTS[part]
            act.wait_ge(s[f"w{part}_loaded"], 16)
            nc.scalar.copy(w_hi[:, cols], w_in[:, cols]).then_inc(s["hi"], 1)

        split_w(0)

        def prep_t(b):
            act.wait_ge(s["xt"], b + 1)
            need(act, s["qkp"], PAIRS * b)
            need(act, s["vp"], 4 * b)
            nc.scalar.copy(xt_hi[:, :], VY[:, 0:N]).then_inc(s["xth"], 1)

        def copy_v(b, par, c):
            act.wait_ge(s["vp"], 4 * b + c + 1)
            need(act, s["ot"], PAIRS * (b - 1))
            nc.scalar.copy(v[par][:, c // 2, 512 * (c % 2):512 * (c % 2) + 512], VY[:, :]).then_inc(s["vs"], 1)

        def exps(b, h):
            act.wait_ge(s["mx"], H * b + h + 1)
            need(act, s["tr"], H * b + h - 7)
            for t in range(NH):
                last = nc.scalar.activation(prob[h % 8][:, t, :], S[h % 2][:, N * t:N * t + N], ACT.Exp,
                                            bias=shift[:, h % 4, t:t + 1], accum_out=total[:, h % 4, t:t + 1])
            last.then_inc(s["ex"], 1)

        def copy_p(b, h):
            act.wait_ge(s["tr"], H * b + h + 1)
            need(act, s["ot"], PAIRS * b + h // 2 - 1)
            nc.scalar.copy(prob_t[h % 4][:, :, :], PT[h % 2][:, :].rearrange("p (k q) -> p k q", k=NH)).then_inc(s["pt"], 1)

        def split_hi(b, p):
            act.wait_ge(s["qk"], PAIRS * b + p + 1)
            need(act, s["sc"], H * (b - 1) + 2 * p + 2)
            nc.scalar.copy(qk_hi[:, p, :], qk[p % 2][:, :]).then_inc(s["qh"], 1)

        prep_t(0)
        split_w(1)
        split_w(2)
        for p in range(4):
            split_hi(0, p)
            copy_v(0, 0, p)

        def iteration(b, par, attend, prep):
            for step in range(H if attend else DRAIN):
                if step == X_STEP + 1 and prep:
                    prep_t(b + 1)
                if (pq := projected(b, step, LH, prep)) is not None:
                    split_hi(*pq)
                if attend:
                    exps(b, step)
                if (nh := due(b, step, LT, attend)) is not None:
                    copy_p(*nh)
                if step in V_STEPS and prep:
                    copy_v(b + 1, 1 - par, V_STEPS.index(step))
        stepper(act, iteration)

    @blk.vector
    def _(dve):

        def prep_a(b):
            chain = Chain(dve, s["prep"], 3, b)
            need(dve, s["xb"], b)
            stats_tiles(nc, dve, chain, x, b, stat, mv, gate).then_inc(s["mv"], 1)
            chain.close()

        def prep_n(b):
            dve.wait_ge(s["rstd"], b + 1)
            need(dve, s["xt"], b)
            norm_tiles(nc, x, b, mv, rstd, xn).then_inc(s["xn"], 1)

        def prep_b(b):
            dve.wait_ge(s["xth"], b + 1)
            nc.vector.tensor_tensor(xt_lo[:, :], VY[:, 0:N], xt_hi[:, :].bitcast(F32), ALU.subtract).then_inc(s["xtl"], 1)

        def rotate(b, p, bank=QK):
            dve.wait_ge(s["qkp"], PAIRS * b + p + 1)
            need(dve, s["qk"], PAIRS * b + p - 1)
            nc.vector.tensor_tensor(scaled[p % 2][:, :], bank[:, :], turn_c[:, :], ALU.mult)
            nc.vector.stream_shuffle(swapped[p % 2][:, :], bank[:, :], [i ^ 1 for i in range(32)]).then_inc(s["sw"], 1)

        def split_lo(b, p):
            dve.wait_ge(s["qh"], PAIRS * b + p + 1)
            nc.vector.tensor_tensor(qk_lo[:, p, :], qk[p % 2][:, :], qk_hi[:, p, :].bitcast(F32),
                                    ALU.subtract).then_inc(s["ql"], 1)

        def greatest(b, h):
            dve.wait_ge(s["sc"], H * b + h + 1)
            need(dve, s["ex"], H * b + h - 3)
            nc.vector.tensor_reduce(shift[:, h % 4, :], S[h % 2][:, :].rearrange("p (t k) -> p t k", t=NH), AX.X,
                                    ALU.max, negate=True).then_inc(s["mx"], 1)

        def inverse(b, h):
            dve.wait_ge(s["ex"], H * b + h + 1)
            if h % 2 == 0:
                need(dve, s["sc_even"], H * b + h - 2)
            nc.vector.reciprocal(r_sum[:, h % 4, :], total[:, h % 4, :]).then_inc(s["rc"], 1)

        def scale(b, h):
            dve.wait_ge(s["rc"], H * b + h + 1)
            for t in range(NH):
                last = nc.vector.tensor_scalar(prob[h % 8][:, t, :], prob[h % 8][:, t, :], r_sum[:, h % 4, t:t + 1], None,
                                               ALU.mult)
            last.then_inc(s["sc_odd"], 2)

        def copy_o(b, p):
            dve.wait_ge(s["ot"], PAIRS * b + p + 1)
            if p == 0:
                need(dve, s["y"], b)
            nc.vector.tensor_copy(o_t[:, p, :], OT[p % 2][:, 0:N]).then_inc(s["o"], 1)

        prep_a(0)
        prep_n(0)
        def split_w(part):
            cols = W_PARTS[part]
            dve.wait_ge(s["hi"], part + 1)
            nc.vector.tensor_tensor(w_lo[:, cols], w_in[:, cols], w_hi[:, cols].bitcast(F32), ALU.subtract).then_inc(s["split"], 1)

        split_w(0)
        prep_b(0)
        split_w(1)
        dve.wait_ge(s["c_loaded"], 64)
        for p in range(PAIRS - 3):
            rotate(0, p, (QK, OT[1])[p % 2])
            if p:
                split_lo(0, p - 1)
            else:
                split_w(2)

        def iteration(b, par, attend, prep):
            for step in range(H if attend else DRAIN):
                if attend:
                    greatest(b, step)
                if step == Y_STEP + 1 and not (isinstance(b, int) and b == 0):
                    dve.wait_ge(s["y"], b)
                    dve.wait_ge(s["xb"], b)
                    tiles = bass.ds(2 * (b - 1), 2)
                    nc.vector.tensor_tensor(x[:, tiles, :], x[:, tiles, :], VY[:, 0:N].rearrange("p (t d) -> p t d", t=NH),
                                            ALU.add).then_inc(s["xadd"], 1)
                if step == X_STEP + 1 and prep:
                    prep_b(b + 1)
                if (pq := projected(b, step, LR, prep)) is not None:
                    rotate(*pq, OT[1] if isinstance(b, int) and b == 0 and step == 0 else QK)
                if (nh := due(b, step, LI, attend)) is not None:
                    inverse(*nh)
                if (nh := due(b, step, LS, attend)) is not None and nh[1] % 2:
                    scale(*nh)
                if (nh := due(b, step, LO, attend)) is not None and nh[1] % 2:
                    copy_o(nh[0], nh[1] // 2)
                if (pq := projected(b, step, LH, prep)) is not None:
                    split_lo(*pq)
                if prep and step == 0:
                    prep_a(b + 1)
                if prep and step == 2:
                    prep_n(b + 1)
        stepper(dve, iteration)


def distance_buckets():
    hot = np.zeros((33, 384), np.float32)
    for u in range(384):
        n = 127 - u + 128
        if n < 0:
            hot[32, u] = 1.0
        elif n < 16:
            hot[n, u] = 1.0
        else:
            hot[min(16 + int(math.log(n / 16) / math.log(8) * 16 + 1e-9), 31), u] = 1.0
    return hot


def load_constants(nc, x, x_in, ident, ident_in, with_x):
    with nc.semaphore("ident_loaded") as loaded, nc.Block() as blk:
        @blk.sync
        def _(sp):
            sp.dma_start(ident[:, :], ident_in).then_inc(loaded, 16)
            if with_x:
                sp.dma_start(x[:, :, :], x_in.rearrange("b (t p) d -> p (b t) d", p=128)).then_inc(loaded, 16)
            sp.wait_ge(loaded, 32 if with_x else 16)


def store(nc, x, out):
    with nc.semaphore("stored") as stored, nc.Block() as blk:
        @blk.sync
        def _(sp):
            sp.dma_start(out.rearrange("b (t p) d -> p (b t) d", p=128), x[:, :, :]).then_inc(stored, 16)
            sp.wait_ge(stored, 16)


def build(nc, t, out, parts=("a", "f1", "b", "f2")):
    with ExitStack() as top:
        x = top.enter_context(nc.sbuf_tensor("tokens", [128, NT, D], F32))
        ident = top.enter_context(nc.sbuf_tensor("identity", [128, 128], F32))
        load_constants(nc, x, t["x"], ident, t["ident"], parts[0] != "a")
        for part in parts:
            if part == "a":
                with ExitStack() as ctx:
                    causal_attention(nc, ctx, x, ident, t["x"], t["a_wq"], t["a_wk"], t["a_wv"], t["a_wo"], t["a_bo"],
                                     t["rel_emb"], t["buckets"])
            elif part == "b":
                with ExitStack() as ctx:
                    rotary_attention(nc, ctx, x, ident, t["b_wqk"], t["b_wv"], t["b_wout"], t["b_bout"], t["cos"], t["sin"])
            else:
                expert_choice_ffn(nc, part + "_", x, ident, t["gate_w"], t["wg"], t["wu"], t["wd"], t["ws_g"], t["ws_u"],
                                  t["ws_d"], t["slots"])
        store(nc, x, out)


def rotation():
    angle = (np.arange(N, dtype=np.float32)[:, None] *
             (np.float32(1.0) / np.float32(10000.0) ** (np.arange(0, 32, 2, dtype=np.float32) / np.float32(32)))[None, :])
    cos, sin = np.ones((2, 64, N), np.float32), np.zeros((2, 64, N), np.float32)
    for d in range(32):
        cos[:, d] = np.cos(angle[:, d // 2])
        sin[:, d] = np.sin(angle[:, d // 2]) * (1 if d % 2 else -1)
    cos, sin = cos.reshape(128, N), sin.reshape(128, N)
    scale = np.float32(64 ** -0.5)
    return np.concatenate([cos * scale, cos], 1), np.concatenate([sin * scale, sin], 1)


def constants():
    cos, sin = rotation()
    return {"ident": np.eye(128, dtype=np.float32), "buckets": distance_buckets(), "cos": cos, "sin": sin,
            "slots": np.arange(1, 33, dtype=np.float32)}


def laid_out(i):
    A, B, Fn = "L0_attn_a_", "L0_attn_b_", "L0_ffn_"
    swap = lambda a: np.ascontiguousarray(np.swapaxes(a, -1, -2))
    wq, wk, wv = i[B + "Wq"], i[B + "Wkv"][:, :1024], i[B + "Wkv"][:, 1024:]
    wqk = np.stack([wq.reshape(D, 8, 128), wk.reshape(D, 8, 128)], 2).reshape(D, 2048)
    return {"b_wqk": wqk, "b_wv": np.ascontiguousarray(wv), "b_wout": i[B + "Wout"], "b_bout": i[B + "bout"],
            "x": i[A + "x"], "a_wq": i[A + "Wq"], "a_wk": i[A + "Wk"], "a_wv": i[A + "Wv"], "a_wo": i[A + "Wo"],
            "a_bo": i[A + "bo"], "rel_emb": i[A + "rel_emb"],
            "gate_w": swap(i[Fn + "gate_w"]), "wg": swap(i[Fn + "Wg"]), "wu": swap(i[Fn + "Wu"]), "wd": swap(i[Fn + "Wd"]),
            "ws_g": swap(i[Fn + "Ws_g"]), "ws_u": swap(i[Fn + "Ws_u"]), "ws_d": swap(i[Fn + "Ws_d"])}


def kernel(**inputs):
    from concourse import bacc
    from concourse.bass_utils import run_bass_kernel_spmd

    nc = bacc.Bacc("TRN2", target_bir_lowering=False, num_devices=1)
    arrays = {n: np.ascontiguousarray(a) for n, a in {**laid_out(inputs), **constants()}.items()}
    tensors = {n: nc.dram_tensor(n, a.shape, mybir.dt.from_np(a.dtype), kind="ExternalInput").ap()
               for n, a in arrays.items()}
    out = nc.dram_tensor("out", (NB, N, D), F32, kind="ExternalOutput").ap()
    build(nc, tensors, out)
    return run_bass_kernel_spmd(nc, [arrays], core_ids=[0]).results[0]["out"]
```
